# Optimizing a Trainium2 kernel written in Bass

```python
import numpy as np
import jax
import jax.numpy as jnp

def _softmax(x, axis=-1):
    return jax.nn.softmax(x, axis=axis)

def _gelu(x):
    return jax.nn.gelu(x, approximate=True)

def _silu(x):
    return jax.nn.silu(x)

def _sigmoid(x):
    return jax.nn.sigmoid(x)

def _layernorm(x, axis=-1, eps=1e-05):
    m = jnp.mean(x, axis=axis, keepdims=True)
    v = jnp.var(x, axis=axis, keepdims=True)
    return (x - m) / jnp.sqrt(v + eps)

def _scatter_add(tgt, idx, src, axis=0):
    return tgt.at[idx].add(src)

def _segment_sum(src, seg, n):
    return jax.ops.segment_sum(src, seg, n)
kernel_name = 'mk_gnn_resnorm_d1_gnn_r32_dab537'

def setup_inputs(seed: int=0):
    np.random.seed(seed)
    _w = jnp.asarray

    def _rec_inputs():
        import jax
        import jax.numpy as jnp
        _gk = jax.random.key(seed)
        x = -0.000364 + 1 * jax.random.normal(jax.random.fold_in(_gk, 1), (625, 768), jnp.float32)
        src = jax.random.randint(jax.random.fold_in(_gk, 2), (10000,), 0, 625, jnp.int32)
        dst = jax.random.randint(jax.random.fold_in(_gk, 3), (10000,), 0, 625, jnp.int32)
        _o = jnp.argsort(dst, stable=True)
        src = src[_o]
        dst = dst[_o]
        return (x, src, dst)
    x, src, dst = _rec_inputs()

    def _L0_gnn_setup():
        import jax, jax.numpy as jnp
        import numpy as np
        N, E, DIM, HEADS = (625, 10000, 768, 8)
        HD = DIM // HEADS
        EPS = 1e-05

        def layer_norm(x, w, b):
            mu = jnp.mean(x, axis=-1, keepdims=True)
            var = jnp.var(x, axis=-1, keepdims=True)
            return (x - mu) * jax.lax.rsqrt(var + EPS) * w + b

        def gatv2(x, src, dst, Ws, bs, Wd, bd, attn):
            H, D = attn.shape
            fs = (x @ Ws + bs).reshape(-1, H, D)
            fd = (x @ Wd + bd).reshape(-1, H, D)
            e = jax.nn.leaky_relu(fs[src] + fd[dst], 0.2)
            logits = jnp.einsum('ehd,hd->eh', e, attn)
            m = jax.ops.segment_max(logits, dst, num_segments=N)
            ex = jnp.exp(logits - m[dst])
            denom = jax.ops.segment_sum(ex, dst, num_segments=N)
            alpha = ex / denom[dst]
            out = jax.ops.segment_sum(alpha[:, :, None] * fs[src], dst, num_segments=N)
            return jax.nn.elu(out)
        key = jax.random.key(seed)
        ks = jax.random.split(key, 10)
        s = 1.0 / np.sqrt(DIM)
        return {'x': jax.random.normal(ks[0], (N, DIM), jnp.float32), 'src': jax.random.randint(ks[1], (E,), 0, N, jnp.int32), 'dst': jax.random.randint(ks[2], (E,), 0, N, jnp.int32), 'W1s': jax.random.normal(ks[3], (DIM, DIM), jnp.float32) * s, 'b1s': jnp.zeros((DIM,), jnp.float32), 'W1d': jax.random.normal(ks[4], (DIM, DIM), jnp.float32) * s, 'b1d': jnp.zeros((DIM,), jnp.float32), 'attn1': jax.random.normal(ks[5], (HEADS, HD), jnp.float32) * s, 'ln1_w': jnp.ones((DIM,), jnp.float32), 'ln1_b': jnp.zeros((DIM,), jnp.float32), 'Wos': jax.random.normal(ks[6], (DIM, DIM), jnp.float32) * s, 'bos': jnp.zeros((DIM,), jnp.float32), 'Wod': jax.random.normal(ks[7], (DIM, DIM), jnp.float32) * s, 'bod': jnp.zeros((DIM,), jnp.float32), 'attno': jax.random.normal(ks[8], (1, DIM), jnp.float32) * s, 'lno_w': jnp.ones((DIM,), jnp.float32), 'lno_b': jnp.zeros((DIM,), jnp.float32)}
    _L0_gnn_all = _L0_gnn_setup()
    _L0_gnn_in = {k: v for k, v in _L0_gnn_all.items() if k in ('W1s', 'b1s', 'W1d', 'b1d', 'attn1', 'ln1_w', 'ln1_b', 'Wos', 'bos', 'Wod', 'bod', 'attno', 'lno_w', 'lno_b')}
    del _L0_gnn_all
    return {'x': x, 'src': src, 'dst': dst, 'L0_gnn_W1s': _L0_gnn_in['W1s'], 'L0_gnn_b1s': _L0_gnn_in['b1s'], 'L0_gnn_W1d': _L0_gnn_in['W1d'], 'L0_gnn_b1d': _L0_gnn_in['b1d'], 'L0_gnn_attn1': _L0_gnn_in['attn1'], 'L0_gnn_ln1_w': _L0_gnn_in['ln1_w'], 'L0_gnn_ln1_b': _L0_gnn_in['ln1_b'], 'L0_gnn_Wos': _L0_gnn_in['Wos'], 'L0_gnn_bos': _L0_gnn_in['bos'], 'L0_gnn_Wod': _L0_gnn_in['Wod'], 'L0_gnn_bod': _L0_gnn_in['bod'], 'L0_gnn_attno': _L0_gnn_in['attno'], 'L0_gnn_lno_w': _L0_gnn_in['lno_w'], 'L0_gnn_lno_b': _L0_gnn_in['lno_b']}

def reference(x, src, dst, L0_gnn_W1s, L0_gnn_b1s, L0_gnn_W1d, L0_gnn_b1d, L0_gnn_attn1, L0_gnn_ln1_w, L0_gnn_ln1_b, L0_gnn_Wos, L0_gnn_bos, L0_gnn_Wod, L0_gnn_bod, L0_gnn_attno, L0_gnn_lno_w, L0_gnn_lno_b):
    import jax
    import jax.numpy as jnp

    def _L0_gnn_ref(x, src, dst, W1s, b1s, W1d, b1d, attn1, ln1_w, ln1_b, Wos, bos, Wod, bod, attno, lno_w, lno_b):
        import jax, jax.numpy as jnp
        import numpy as np
        N, E, DIM, HEADS = (625, 10000, 768, 8)
        HD = DIM // HEADS
        EPS = 1e-05

        def layer_norm(x, w, b):
            mu = jnp.mean(x, axis=-1, keepdims=True)
            var = jnp.var(x, axis=-1, keepdims=True)
            return (x - mu) * jax.lax.rsqrt(var + EPS) * w + b

        def gatv2(x, src, dst, Ws, bs, Wd, bd, attn):
            H, D = attn.shape
            fs = (x @ Ws + bs).reshape(-1, H, D)
            fd = (x @ Wd + bd).reshape(-1, H, D)
            e = jax.nn.leaky_relu(fs[src] + fd[dst], 0.2)
            logits = jnp.einsum('ehd,hd->eh', e, attn)
            m = jax.ops.segment_max(logits, dst, num_segments=N)
            ex = jnp.exp(logits - m[dst])
            denom = jax.ops.segment_sum(ex, dst, num_segments=N)
            alpha = ex / denom[dst]
            out = jax.ops.segment_sum(alpha[:, :, None] * fs[src], dst, num_segments=N)
            return jax.nn.elu(out)
        h = gatv2(x, src, dst, W1s, b1s, W1d, b1d, attn1).reshape(N, DIM)
        h = layer_norm(h + x, ln1_w, ln1_b)
        out = gatv2(h, src, dst, Wos, bos, Wod, bod, attno).reshape(N, DIM)
        return layer_norm(out, lno_w, lno_b)
    x = _layernorm(x + _L0_gnn_ref(x, src, dst, L0_gnn_W1s, L0_gnn_b1s, L0_gnn_W1d, L0_gnn_b1d, L0_gnn_attn1, L0_gnn_ln1_w, L0_gnn_ln1_b, L0_gnn_Wos, L0_gnn_bos, L0_gnn_Wod, L0_gnn_bod, L0_gnn_attno, L0_gnn_lno_w, L0_gnn_lno_b), axis=-1)
    return x

_drawn_inputs = setup_inputs


def setup_inputs(seed=0):
    import zlib

    import numpy as np

    out = dict(_drawn_inputs(seed))
    spreads = {'L0_gnn_b1s': (0.0, 0.1),
     'L0_gnn_b1d': (0.0, 0.8),
     'L0_gnn_ln1_w': (1.0, 0.2),
     'L0_gnn_ln1_b': (0.0, 0.1),
     'L0_gnn_bos': (0.0, 0.1),
     'L0_gnn_bod': (0.0, 0.472),
     'L0_gnn_lno_w': (1.0, 0.2),
     'L0_gnn_lno_b': (0.0, 0.1)}
    factors = {'L0_gnn_W1d': 3.249}
    for name, (base, spread) in spreads.items():
        noise = np.random.default_rng([zlib.crc32(name.encode()), seed]).standard_normal(out[name].shape)
        drawn = base * np.exp(spread * noise) if base else spread * noise
        out[name] = jnp.asarray(drawn.astype(out[name].dtype))
    for name, factor in factors.items():
        out[name] = (out[name] * factor).astype(out[name].dtype)
    return out
```

```python
from contextlib import ExitStack

import concourse.bass as bass
from concourse import mybir

ALU = mybir.AluOpType
ACT = mybir.ActivationFunctionType
AX_X = mybir.AxisListType.X
F32 = mybir.dt.float32
BF16 = mybir.dt.bfloat16
I32 = mybir.dt.int32

P = 128
NODES, EDGES, DIM, HEADS = 625, 10000, 768, 8
HD = DIM // HEADS
HALF = DIM // 2
KC = DIM // P
CHUNKS = -(-NODES // P)
LAST = NODES - (CHUNKS - 1) * P
TILES = 84
GROUPS = 6
GT = 16
TPAD = GROUPS * GT
ROW = DIM + HEADS
UN = 4
TURNS = TILES // UN
QW = 256
DEN = CHUNKS * DIM
SLOTS = TPAD * P
STAGE = EDGES + SLOTS
SLOT_LEN = P + TILES * P + SLOTS
PAD_DST = 1000.0
NO = -1.0e30
EPS = 1e-5
SLOPE = 0.2
SORT_SHIFT = 16384.0
ETILES = -(-EDGES // P)
RB = 1264
RBLOCKS = ETILES * P // RB
TINY = 1e-30


def gat_kernel(nc, x, src, dst, w1s, b1s, w1d, b1d, attn1, ln1w, ln1b,
               wos, bos, wod, bod, attno, lnow, lnob, out):
    staged = nc.dram_tensor("staged_edges", [2, STAGE], I32, kind="Internal").ap()
    slots = nc.dram_tensor("edge_slots", [2, SLOT_LEN], I32, kind="Internal").ap()
    tables = [nc.dram_tensor(f"fs_table{l}", [NODES, ROW], F32, kind="Internal").ap() for l in range(2)]

    with ExitStack() as ctx:
        def sb(name, shape, dt):
            return ctx.enter_context(nc.sbuf_tensor(name, shape, dt))

        def sem(name):
            return ctx.enter_context(nc.semaphore(name))

        x_sb = sb("x_sb", [P, CHUNKS, DIM], F32)
        actT = sb("actT", [P, KC, CHUNKS * P], F32)
        w_s = sb("w_s", [P, KC, DIM], F32)
        w_d = sb("w_d", [P, KC, DIM], F32)
        attn = sb("attn", [P, DIM], F32)
        vec = [sb(f"vec{i}", [P, DIM], F32) for i in range(2)]
        bias_s, bias_d = vec
        ln_w, ln_b = vec
        fd3 = sb("fd3", [P, CHUNKS, 3, ROW], BF16)
        ohT = sb("ohT", [P, TILES, P], BF16)
        arena = sb("arena", [P, TILES * P], F32)
        ident = sb("ident", [P, P], F32)
        ones = sb("ones", [P, P], F32)
        iota_f = sb("iota_f", [P, P], F32)
        iota_t = sb("iota_t", [P, TPAD], F32)
        iota_128k = sb("iota_128k", [P, 80], F32)
        iota_p = sb("iota_p", [P, 1], F32)
        zero_w = sb("zero_w", [P, P], BF16)
        zero_m = sb("zero_m", [P, 512], BF16)
        pads = sb("pads", [P, 2, SLOTS // P], I32)
        keys_i = sb("keys_i", [P, 81], I32)
        keys = sb("keys", [P, 81], F32)
        scrap = sb("scrap", [P, 128], F32)
        stat = sb("stat", [P, 5], F32)
        cnt = sb("cnt", [P, 5], F32)
        flag_i = sb("flag_i", [P, 1], I32)
        off = sb("off", [P, 6], F32)
        seg_n = sb("seg_n", [P, 5], F32)
        seg_t = sb("seg_t", [P, 5], F32)
        tile0 = sb("tile0", [P, 6], F32)
        off_i = sb("off_i", [P, 6], I32)
        tile0_i = sb("tile0_i", [P, 6], I32)
        ct = sb("ct", [P, TPAD], F32)
        ct_i = sb("ct_i", [P, TPAD], I32)
        node_no = sb("node_no", [P, TPAD], F32)
        rows_i = sb("rows_i", [TPAD, 2, P], I32)
        rows_f = sb("rows_f", [TPAD, 2, P], F32)
        src_i = sb("src_i", [P, TPAD], I32)
        dst_rel = sb("dst_rel", [P, TPAD], F32)
        spread = sb("spread", [GT, GT, HEADS], F32)
        pen = sb("pen", [P, 4, GROUPS, P], BF16)
        ends_i = sb("ends_i", [1, 2, TPAD], I32)
        ends = sb("ends", [1, 2, TPAD], F32)
        single = sb("single", [1, TPAD], F32)
        cont = sb("cont", [1, TPAD], F32)
        tmp_row = sb("tmp_row", [1, TPAD], F32)
        chain_pen = sb("chain_pen", [1, 4, TPAD], F32)
        chain_a = sb("chain_a", [1, 2, HEADS, TPAD], BF16)
        relu_sum = sb("relu_sum", [P, TPAD, HEADS], F32)
        lin = sb("lin", [P, TPAD, HEADS], F32)
        logits = sb("logits", [P, TPAD, HEADS], F32)
        ex = sb("ex", [P, TPAD, HEADS], F32)
        e16_i = logits[0:GT, :, :].rearrange("p t h -> p (t h)").bitcast(I32)
        e16 = ex[0:GT, :, :].rearrange("p t h -> p (t h)")
        idx_now = sb("idx_now", [P, UN], I32)
        rden = sb("rden", [P, CHUNKS * HEADS], F32)
        bn6 = sb("bn6", [P, CHUNKS, 2, 6], F32)
        mv = sb("mv", [P, CHUNKS, 2], F32)
        var_e = sb("var_e", [P, CHUNKS], F32)
        root = sb("root", [P, CHUNKS], F32)
        rstd = sb("rstd", [P, CHUNKS], F32)
        nt1 = sb("nt1", [P, CHUNKS], F32)

        ps = ctx.enter_context(nc.psum_tensor("ps", [P, 4096], F32))

        def part(at, *shape):
            n = 1
            for s in shape:
                n *= s
            v = arena[:, at:at + n]
            if len(shape) == 2:
                return v.rearrange("p (a b) -> p a b", a=shape[0])
            if len(shape) == 3:
                return v.rearrange("p (a b c) -> p a b c", a=shape[0], b=shape[1])
            return v

        dst_bc = arena[:, :].bitcast(I32).rearrange("p (t e) -> p t e", t=TILES)
        stage_f = sb("stage_f", [P, 2, ROW], F32)
        prod = sb("prod", [P, DIM], F32)
        dst_ht = prod[:, :].rearrange("p (g e) -> p g e", g=GROUPS)
        gat = part(0, UN, ROW)
        sums = part(UN * ROW, 2, HALF + HEADS)
        prods = part(UN * ROW + 2 * (HALF + HEADS), 2, DIM)
        at_oh = UN * ROW + 2 * (HALF + HEADS) + 2 * DIM
        onehot = part(at_oh, 2, P)
        at_p2 = at_oh + 2 * P
        lt = part(0, GROUPS, P)
        mx = part(DIM, GROUPS, P)
        mx2 = part(2 * DIM, GROUPS, P)
        mrow = part(3 * DIM, 2, DIM)
        brow = part(5 * DIM, 2, DIM)
        srow = part(7 * DIM, 2, DIM)
        carry = part(9 * DIM, 2 * GROUPS)
        v_sb = part(0, CHUNKS, DIM)
        neg = part(CHUNKS * DIM, 2, DIM)
        posm = part((CHUNKS + 2) * DIM, 2, DIM)
        rk_int = arena[:, 0:RB].bitcast(I32)
        rk_key = arena[:, RB:2 * RB]
        rk_iota = arena[:, 2 * RB:3 * RB]
        rk_out = arena[:, 3 * RB:4 * RB]
        rk_cnt = arena[:, 4 * RB:4 * RB + RBLOCKS * ETILES]
        at_rk = 4 * RB + RBLOCKS * ETILES
        rk_col_i = arena[:, at_rk:at_rk + 2 * ETILES].bitcast(I32).rearrange("p (a t) -> p a t", a=2)
        rk_eno = arena[:, at_rk + 2 * ETILES:at_rk + 3 * ETILES]
        rk_kcol = arena[:, at_rk + 3 * ETILES:at_rk + 4 * ETILES]
        rk_pos = arena[:, at_rk + 4 * ETILES:at_rk + 5 * ETILES]
        rk_pos_i = arena[:, at_rk + 5 * ETILES:at_rk + 7 * ETILES].bitcast(I32).rearrange("p (a t) -> p a t", a=2)
        rk_idx = arena[:, at_rk + 7 * ETILES:at_rk + 7 * ETILES + 2].bitcast(I32)
        rk_val = arena[:, at_rk + 7 * ETILES + 2:at_rk + 7 * ETILES + 4].bitcast(I32)

        pads_set = sem("pads_set")
        consts_set = sem("consts_set")
        ident_set = sem("ident_set")
        staged_in = sem("staged_in")
        keys_in = sem("keys_in")
        stats_ready = sem("stats_ready")
        counts_ready = sem("counts_ready")
        flag_ready = sem("flag_ready")
        rank_cols = sem("rank_cols")
        rank_blk = sem("rank_blk")
        rank_used = sem("rank_used")
        rank_iota = sem("rank_iota")
        ranked = sem("ranked")
        rank_tile = sem("rank_tile")
        rank_copy = sem("rank_copy")
        rank_out = sem("rank_out")
        edges_sorted = sem("edges_sorted")
        tile_tables = sem("tile_tables")
        slots_made = sem("slots_made")
        rows_in = sem("rows_in")
        e16_in = sem("e16_in")
        ends_in = sem("ends_in")
        dstbc_in = sem("dstbc_in")
        rows_conv = sem("rows_conv")
        rows_turned = sem("rows_turned")
        src_ready = sem("src_ready")
        e16_conv = sem("e16_conv")
        dst_spread = sem("dst_spread")
        ohT_ready = sem("ohT_ready")
        x_in = sem("x_in")
        w_in = sem("w_in")
        bias_in = sem("bias_in")
        norm_in = sem("norm_in")
        attn_in = sem("attn_in")
        turned = [sem(f"turned{b}") for b in range(2)]
        turn_copied = [sem(f"turn_copied{b}") for b in range(2)]
        proj_ready = [sem(f"proj_ready{b}") for b in range(2)]
        proj_free = [sem(f"proj_free{b}") for b in range(2)]
        row_ready = [sem(f"row_ready{b}") for b in range(2)]
        table_stored = sem("table_stored")
        fd_ready = sem("fd_ready")
        fd_part = sem("fd_part")
        gathered = [sem(f"gathered{u}") for u in range(UN)]
        g_free = [sem(f"g_free{u}") for u in range(UN)]
        idx_set = sem("idx_set")
        f_ready = [sem(f"f_ready{b}") for b in range(2)]
        f_free = [sem(f"f_free{b}") for b in range(2)]
        sum_ready = [sem(f"sum_ready{b}") for b in range(2)]
        lin_kept = [sem(f"lin_kept{b}") for b in range(2)]
        prod_ready = [sem(f"prod_ready{b}") for b in range(2)]
        reduced = sem("reduced")
        logits_ready = sem("logits_ready")
        logits_turned = sem("logits_turned")
        lt_ready = sem("lt_ready")
        tile_max = sem("tile_max")
        ends_turned = sem("ends_turned")
        chain_ready = sem("chain_ready")
        chain_spread = sem("chain_spread")
        shifted = sem("shifted")
        exped = sem("exped")
        ex_turned = sem("ex_turned")
        ex_ready = sem("ex_ready")
        zeros_set = sem("zeros_set")
        agg_in = [sem(f"agg_in{b}") for b in range(2)]
        agg_free = [sem(f"agg_free{b}") for b in range(2)]
        agg_done = sem("agg_done")
        normed = sem("normed")
        neg_ready = sem("neg_ready")
        neg_exp = sem("neg_exp")
        pos_ready = sem("pos_ready")
        elu_used = sem("elu_used")
        var_ready = sem("var_ready")
        root_ready = sem("root_ready")
        h_ready = sem("h_ready")
        out_ready = sem("out_ready")
        out_stored = sem("out_stored")
        dve_step = sem("dve_step")

        TURN_PS = [2048, 2560]
        E_PS = [3584, 2048]
        SRC_PS, DST_PS, CNT_PS = 3072, 3200, 3984

        block = ctx.enter_context(nc.Block())

        @block.sync
        def _(sp):
            sp.wait_ge(pads_set, 3)
            for a, v in enumerate((src, dst)):
                sp.dma_start(staged[a, 0:EDGES].rearrange("(b n) -> b n", b=16),
                             v.rearrange("(b n) -> b n", b=16)).then_inc(staged_in, 16)
                sp.dma_start(staged[a, EDGES:STAGE].rearrange("(p n) -> p n", p=P),
                             pads[:, a, :]).then_inc(staged_in, 16)
            sp.wait_ge(staged_in, 64)
            sp.dma_start(keys_i[0:125, 0:80],
                         staged[1, 0:EDGES].rearrange("(p n) -> p n", p=125)).then_inc(keys_in, 16)
            with nc.allow_non_contiguous_dma("the first key of the next partition"):
                sp.dma_start(keys_i[0:125, 80:81],
                             staged[1, 80:80 + EDGES].rearrange("(p n) -> p n", p=125)[:, 0:1]
                             ).then_inc(keys_in, 16)
            sp.wait_ge(edges_sorted, 1)
            sp.wait_ge(tile_tables, 1)
            for c in range(CHUNKS):
                if c == 0:
                    to, frm = P, 0
                else:
                    sp.wait_ge(slots_made, 32 * c)
                    frm = sp.value_load(off_i[0:1, c:c + 1], min_val=0, max_val=EDGES)
                    to = sp.value_load(tile0_i[0:1, c:c + 1], min_val=0, max_val=TILES) * P + P
                for a in range(2):
                    sp.dma_start(slots[a, bass.ds(to, SLOTS)].rearrange("(b n) -> b n", b=16),
                                 staged[a, bass.ds(frm, SLOTS)].rearrange("(b n) -> b n", b=16)
                                 ).then_inc(slots_made, 16)
            sp.wait_ge(slots_made, 32 * CHUNKS)
            for a in range(2):
                sp.dma_start(rows_i[:, a, :], slots[a, P:P + SLOTS].rearrange("(t e) -> t e", e=P)
                             ).then_inc(rows_in, 16)
            sp.dma_start(e16_i.rearrange("t (g e) -> t g e", g=GROUPS),
                         slots[1, P:P + SLOTS].rearrange("(g t e) -> t g e", g=GROUPS, t=GT)
                         ).then_inc(e16_in, 16)
            with nc.allow_non_contiguous_dma("first and last edge of each tile"):
                for a, e in ((0, 0), (1, P - 1)):
                    sp.dma_start(ends_i[0:1, a, :], slots[1, P + e:P + e + SLOTS]
                                 .rearrange("(a t e) -> a t e", a=1, e=P)[:, :, 0]).then_inc(ends_in, 16)
            sp.dma_start(arena[:, :].bitcast(I32),
                         slots[1, P:P + TILES * P].partition_broadcast(P)).then_inc(dstbc_in, 16)
            for l in range(2):
                for c in range(CHUNKS):
                    n = P if c < CHUNKS - 1 else LAST
                    sp.wait_ge(row_ready[0], 5 * l + c + 1)
                    sp.dma_start(tables[l][c * P:c * P + n, :], stage_f[0:n, 0, :]).then_inc(table_stored, 16)
                if l == 0:
                    sp.wait_ge(fd_ready, 2 * CHUNKS)
                    sp.dma_start(w_s[:, :, :], wos.rearrange("(k p) n -> p k n", p=P)).then_inc(w_in, 16)
                    sp.dma_start(w_d[:, :, :], wod.rearrange("(k p) n -> p k n", p=P)).then_inc(w_in, 16)
                    sp.dma_start(ln_w[:, :], ln1w.partition_broadcast(P)).then_inc(norm_in, 16)
                    sp.dma_start(ln_b[:, :], ln1b.partition_broadcast(P)).then_inc(norm_in, 16)
                    sp.wait_ge(logits_ready, 1)
                    sp.dma_start(attn[:, :], attno.rearrange("h d -> (h d)").partition_broadcast(P)
                                 ).then_inc(attn_in, 16)
                    sp.wait_ge(h_ready, CHUNKS)
                    sp.dma_start(bias_s[:, :], bos.partition_broadcast(P)).then_inc(bias_in, 16)
                    sp.dma_start(bias_d[:, :], bod.partition_broadcast(P)).then_inc(bias_in, 16)
                else:
                    sp.wait_ge(fd_ready, 4 * CHUNKS)
                    sp.dma_start(ln_w[:, :], lnow.partition_broadcast(P)).then_inc(norm_in, 16)
                    sp.dma_start(ln_b[:, :], lnob.partition_broadcast(P)).then_inc(norm_in, 16)
            for c in range(CHUNKS):
                n = P if c < CHUNKS - 1 else LAST
                sp.wait_ge(out_ready, c + 1)
                sp.dma_start(out[c * P:c * P + n, :], v_sb[0:n, c, :]).then_inc(out_stored, 16)
            sp.wait_ge(out_stored, 16 * CHUNKS)

        @block.gpsimd
        def _(pool):
            nc.gpsimd.memset(pads[:, 0, :], 0).then_inc(pads_set, 1)
            nc.gpsimd.memset(pads[:, 1, :], int(PAD_DST)).then_inc(pads_set, 1)
            nc.gpsimd.memset(x_sb[:, CHUNKS - 1, :], 0.0).then_inc(pads_set, 1)
            for dstt, pattern, mult in ((iota_f[:, :], [[1, P]], 0), (iota_p[:, :], [[1, 1]], 1),
                                        (iota_t[:, :], [[1, TPAD]], 0), (iota_128k[:, :], [[P, 80]], 0)):
                nc.gpsimd.iota(dstt, pattern, base=0, channel_multiplier=mult,
                               allow_small_or_imprecise_dtypes=True).then_inc(consts_set, 1)
            nc.gpsimd.memset(ones[:, :], 1.0).then_inc(consts_set, 1)
            nc.gpsimd.memset(zero_w[:, :], 0.0).then_inc(consts_set, 1)
            nc.gpsimd.memset(zero_m[:, :], 0.0).then_inc(consts_set, 1)
            nc.gpsimd.memset(relu_sum[:, :, :], 0.0).then_inc(consts_set, 1)
            nc.gpsimd.memset(lin[:, :, :], 0.0).then_inc(consts_set, 1)

            pool.wait_ge(flag_ready, 1)
            unsorted = pool.value_load(flag_i[0:1, 0:1], min_val=0, max_val=EDGES)
            with pool.If(unsorted > 0):
                with nc.allow_non_contiguous_dma("edges to columns"):
                    for a in range(2):
                        pool.dma_start(rk_col_i[:, a, :], staged[a, 0:ETILES * P]
                                       .rearrange("(t p) -> p t", p=P)).then_inc(rank_cols, 16)
                nc.gpsimd.iota(rk_iota, [[1, RB]], base=0, channel_multiplier=0,
                               allow_small_or_imprecise_dtypes=True).then_inc(rank_iota, 1)
                nc.gpsimd.iota(rk_eno, [[P, ETILES]], base=0, channel_multiplier=1,
                               allow_small_or_imprecise_dtypes=True).then_inc(rank_iota, 1)
                for b in range(RBLOCKS):
                    if b > 0:
                        pool.wait_ge(rank_used, b)
                    pool.dma_start(rk_int, staged[1, b * RB:(b + 1) * RB].partition_broadcast(P)
                                   ).then_inc(rank_blk, 16)
                pool.wait_ge(ranked, 1)
                with pool.Fori(0, ETILES) as t:
                    for a in range(2):
                        nc.gpsimd.tensor_copy(rk_idx[:, a:a + 1], rk_pos_i[:, a, bass.ds(t, 1)]
                                              ).then_inc(rank_copy, 1)
                        nc.gpsimd.tensor_copy(rk_val[:, a:a + 1], rk_col_i[:, a, bass.ds(t, 1)]
                                              ).then_inc(rank_copy, 1)
                        pool.wait_ge(rank_copy, 4 * t + 2 * a + 2)
                        pool.nop(nofuse=True)
                        nc.gpsimd.indirect_dma_start(
                            out=staged.rearrange("a (n o) -> (a n) o", o=1),
                            out_offset=bass.IndirectOffsetOnAxis(ap=rk_idx[:, a:a + 1], axis=0),
                            in_=rk_val[:, a:a + 1], in_offset=None).then_inc(rank_out, 16)
                        pool.wait_ge(rank_out, 32 * t + (16 * a + 16))
                        pool.nop(nofuse=True)
                pool.wait_ge(rank_out, 32 * ETILES)
                pool.nop(nofuse=True)
            nc.gpsimd.memset(ends[0:1, 0, 0:1], 0.0).then_inc(edges_sorted, 1)

            pool.wait_ge(src_ready, 1)

            def gathers(phase, l):
                pool.wait_ge(table_stored, 16 * CHUNKS * (l + 1))
                if phase % 2 == 0:
                    pool.wait_ge(ohT_ready, 1)
                if phase == 2:
                    pool.wait_ge(h_ready, CHUNKS)
                if phase % 2 == 1:
                    pool.wait_ge(ex_ready, l + 1)
                with pool.Fori(0, TURNS) as i:
                    for u in range(UN):
                        pool.wait_ge(g_free[u], i + (1 + TURNS * phase))
                        pool.nop(nofuse=True)
                        nc.gpsimd.tensor_copy(idx_now[:, u:u + 1], src_i[:, bass.ds(i * UN + u, 1)]
                                              ).then_inc(idx_set, 1)
                        pool.wait_ge(idx_set, i * UN + (u + 1 + TILES * phase))
                        pool.nop(nofuse=True)
                        nc.gpsimd.indirect_dma_start(
                            out=gat[:, u, :], out_offset=None, in_=tables[l],
                            in_offset=bass.IndirectOffsetOnAxis(ap=idx_now[:, u:u + 1], axis=0)
                        ).then_inc(gathered[u], 16)

            for l in range(2):
                gathers(2 * l, l)
                gathers(2 * l + 1, l)
                for c in range(CHUNKS):
                    pool.wait_ge(normed, CHUNKS * l + c + 1)
                    if c >= 2:
                        pool.wait_ge(elu_used, CHUNKS * l + c - 1)
                    nc.gpsimd.tensor_scalar(posm[:, c % 2, :], v_sb[:, c, :], 0.0, -1.0,
                                            ALU.max, ALU.add).then_inc(pos_ready, 1)

        @block.scalar
        def _(act):
            act.wait_ge(pads_set, 3)
            for c in range(CHUNKS):
                n = P if c < CHUNKS - 1 else LAST
                act.dma_start(x_sb[0:n, c, :], x[c * P:c * P + n, :]).then_inc(x_in, 16)
            act.dma_start(w_s[:, :, :], w1s.rearrange("(k p) n -> p k n", p=P)).then_inc(w_in, 16)
            act.dma_start(w_d[:, :, :], w1d.rearrange("(k p) n -> p k n", p=P)).then_inc(w_in, 16)
            act.dma_start(bias_s[:, :], b1s.partition_broadcast(P)).then_inc(bias_in, 16)
            act.dma_start(bias_d[:, :], b1d.partition_broadcast(P)).then_inc(bias_in, 16)
            act.dma_start(attn[:, :], attn1.rearrange("h d -> (h d)").partition_broadcast(P)).then_inc(attn_in, 16)

            for l in range(2):
                for g in range(2 * CHUNKS):
                    c, half = g // 2, g % 2
                    act.wait_ge(turned[g % 2], CHUNKS * l + c + 1)
                    nc.scalar.copy(actT[:, 3 * half:3 * half + 3, c * P:(c + 1) * P],
                                   ps[:, TURN_PS[g % 2]:TURN_PS[g % 2] + 3 * P]
                                   .rearrange("p (k n) -> p k n", k=3)).then_inc(turn_copied[g % 2], 1)
                for c in range(CHUNKS):
                    for k in range(2):
                        act.wait_ge(row_ready[1], 2 * (CHUNKS * l + c) + k + 1)
                        nc.scalar.copy(fd3[:, c, k, :], stage_f[:, 1, :]).then_inc(fd_part, 1)

                with act.Fori(0, TURNS) as i:
                    for u in range(UN):
                        b = u % 2
                        act.wait_ge(sum_ready[b], i * 2 + (u // 2 + 1 + 2 * TURNS * l))
                        nc.scalar.copy(lin[:, bass.ds(i * UN + u, 1), :],
                                       sums[:, b, HALF:HALF + HEADS].rearrange("p (a h) -> p a h", a=1)
                                       ).then_inc(lin_kept[b], 1)
                act.wait_ge(logits_turned, l + 1)
                nc.scalar.mul(lt, ps[:, 0:DIM].rearrange("p (g e) -> p g e", g=GROUPS), 1.0 - SLOPE
                              ).then_inc(lt_ready, 1)
                act.wait_ge(shifted, l + 1)
                nc.scalar.activation(mx2, lt, ACT.Exp).then_inc(exped, 1)
                act.wait_ge(ex_turned, l + 1)
                nc.scalar.copy(ex[:, :, :].rearrange("p t h -> p (t h)"), ps[:, 0:DIM]).then_inc(ex_ready, 1)
                for c in range(CHUNKS):
                    act.wait_ge(neg_ready, CHUNKS * l + c + 1)
                    nc.scalar.activation(neg[:, c % 2, :], neg[:, c % 2, :], ACT.Exp).then_inc(neg_exp, 1)
                act.wait_ge(var_ready, l + 1)
                nc.scalar.sqrt(root[:, :], var_e[:, :]).then_inc(root_ready, 1)
            act.wait_ge(var_ready, 3)
            nc.scalar.sqrt(root[:, :], var_e[:, :]).then_inc(root_ready, 1)

        @block.tensor
        def _(pe):
            for s in agg_free:
                pe.sem_inc(s, 1)
            pe.wait_ge(ident_set, 1)
            pe.wait_ge(x_in, 16 * CHUNKS)

            def turn_input(l, rows):
                for g in range(2 * CHUNKS):
                    c, half = g // 2, g % 2
                    if l > 0 and half == 0:
                        pe.wait_ge(h_ready, c + 1)
                    if c > 0 or l > 0:
                        pe.wait_ge(turn_copied[g % 2], CHUNKS * l + c)
                    for k in range(3):
                        at = TURN_PS[g % 2] + k * P
                        mm = pe.transpose(ps[:, at:at + P], rows[:, c, (3 * half + k) * P:(3 * half + k + 1) * P],
                                          ident[:, :])
                    mm.then_inc(turned[g % 2], 1)

            def project(l, g):
                c, w = g // 2, (w_s, w_d)[g % 2]
                b = g % 2
                if g == 0:
                    pe.wait_ge(w_in, 32 * (l + 1))
                pe.wait_ge(turn_copied[0], CHUNKS * l + c + 1)
                pe.wait_ge(turn_copied[1], CHUNKS * l + c + 1)
                if l > 0 or g >= 2:
                    pe.wait_ge(proj_free[b], CHUNKS * l + c)
                for half in range(2):
                    for k in range(KC):
                        mm = pe.matmul(ps[:, b * 1024 + half * 512:b * 1024 + half * 512 + HALF],
                                       actT[:, k, c * P:(c + 1) * P], w[:, k, half * HALF:(half + 1) * HALF],
                                       start=(k == 0), stop=(k == KC - 1))
                mm.then_inc(proj_ready[b], 1)

            def prepare():
                pe.wait_ge(rows_conv, 1)
                for a, at in ((0, SRC_PS), (1, DST_PS)):
                    mm = pe.transpose(ps[:, at:at + TPAD], rows_f[:, a, :], ident[0:TPAD, 0:TPAD])
                mm.then_inc(rows_turned, 1)
                pe.wait_ge(e16_conv, 1)
                for a in range(2):
                    mm = pe.matmul(ps[:, E_PS[a]:E_PS[a] + HALF],
                                   spread[:, :, :].rearrange("a t h -> a (t h)"),
                                   e16[:, a * HALF:(a + 1) * HALF], start=True, stop=True)
                mm.then_inc(dst_spread, 1)

            def feature_sums(l):
                pe.wait_ge(fd_ready, 2 * CHUNKS * (l + 1))
                pe.wait_ge(ohT_ready, 1)
                pe.wait_ge(tile_tables, 1)
                pe.wait_ge(proj_free[0], CHUNKS * (l + 1))
                pe.wait_ge(proj_free[1], CHUNKS * (l + 1))
                with pe.Fori(0, TURNS) as i:
                    for u in range(UN):
                        b = u % 2
                        c = pe.value_load(ct_i[0:1, bass.ds(i * UN + u, 1)], min_val=0, max_val=CHUNKS - 1)
                        oh = ohT[:, bass.ds(i * UN + u, 1), :].rearrange("p a e -> p (a e)")
                        pe.wait_ge(f_free[b], i * 2 + (u // 2 + 1 + 2 * TURNS * l))
                        for half in range(2):
                            lo, n = half * HALF, HALF + half * HEADS
                            at = b * 1024 + half * 512
                            for k in range(3):
                                mm = pe.matmul(ps[:, at:at + n], oh,
                                               fd3[:, bass.ds(c, 1), k, lo:lo + n].rearrange("p a n -> p (a n)"),
                                               start=(k == 0), stop=(half == 1 and k == 2))
                            if half == 0:
                                pe.wait_ge(gathered[u], i * 16 + (16 + 16 * TURNS * 2 * l))
                                pe.matmul(ps[:, at:at + n], ident[:, :], gat[:, u, 0:HALF],
                                          start=False, stop=True)
                        mm.then_inc(f_ready[b], 1)

            def softmax_turns(l):
                pe.wait_ge(logits_ready, l + 1)
                for g in range(GROUPS):
                    mm = pe.transpose(ps[:, g * P:(g + 1) * P],
                                      logits[:, g * GT:(g + 1) * GT, :].rearrange("p t h -> p (t h)"), ident[:, :])
                mm.then_inc(logits_turned, 1)
                pe.wait_ge(tile_max, l + 1)
                for a, e in ((0, P - 1), (1, 0)):
                    for g in range(GROUPS):
                        at = 1024 * (a + 1) + g * P
                        mm = pe.matmul(ps[0:1, at:at + P], mx2[:, g, e:e + 1], ident[:, :], start=True, stop=True)
                mm.then_inc(ends_turned, 1)
                pe.wait_ge(chain_ready, 2 * (l + 1))
                for a in range(2):
                    for g in range(GROUPS):
                        at = 3072 + a * GROUPS + g
                        row = brow[0:1, a, g * P:(g + 1) * P]
                        mm = pe.matmul(ps[:, at:at + 1], row, ones[0:1, 0:1], start=True, stop=True)
                mm.then_inc(chain_spread, 1)
                pe.wait_ge(exped, l + 1)
                for g in range(GROUPS):
                    mm = pe.transpose(ps[:, g * P:(g + 1) * P], mx2[:, g, :], ident[:, :])
                mm.then_inc(ex_turned, 1)

            def aggregate(l):
                pe.wait_ge(ex_ready, l + 1)
                for bank in range(8):
                    pe.matmul(ps[:, bank * 512:(bank + 1) * 512], zero_w[:, :], zero_m[:, :],
                              start=True, stop=False, skip_group_check=True)
                with pe.Fori(0, TURNS) as i:
                    for u in range(UN):
                        b = u % 2
                        c = pe.value_load(ct_i[0:1, bass.ds(i * UN + u, 1)], min_val=0, max_val=CHUNKS - 1)
                        pe.wait_ge(agg_in[b], i * 2 + (u // 2 + 1 + 2 * TURNS * l))
                        if l == 1:
                            pe.wait_ge(gathered[u], i * 16 + (16 + 16 * TURNS * 3))
                        for q in range(DIM // QW):
                            rhs = prods[:, b, q * QW:(q + 1) * QW] if l == 0 else gat[:, u, q * QW:(q + 1) * QW]
                            mm = pe.matmul(ps[:, bass.ds(c * DIM + q * QW, QW)], onehot[:, b, :], rhs,
                                           start=False, stop=False, skip_group_check=True)
                        mm.then_inc(g_free[u], 1)
                        den = ex[:, bass.ds(i * UN + u, 1), :].rearrange("p a h -> p (a h)") if l == 0 else ones[:, 0:HEADS]
                        pe.matmul(ps[:, bass.ds(c * HEADS + DEN, HEADS)], onehot[:, b, :], den,
                                  start=False, stop=False, skip_group_check=True).then_inc(agg_free[b], 1)
                for bank in range(8):
                    mm = pe.matmul(ps[:, bank * 512:(bank + 1) * 512], zero_w[:, :], zero_m[:, :],
                                   start=False, stop=True, skip_group_check=True)
                mm.then_inc(agg_done, 1)

            turn_input(0, x_sb)
            pe.wait_ge(stats_ready, 1)
            pe.matmul(ps[:, CNT_PS:CNT_PS + 5], ones[0:125, :], stat[0:125, :], start=True, stop=True
                      ).then_inc(counts_ready, 1)
            for g in range(6):
                project(0, g)
            prepare()
            for g in range(6, 2 * CHUNKS):
                project(0, g)
            for l in range(2):
                if l == 1:
                    turn_input(1, v_sb)
                    for g in range(2 * CHUNKS):
                        project(1, g)
                feature_sums(l)
                softmax_turns(l)
                aggregate(l)

        @block.vector
        def _(dve):
            steps = [0]

            def link(ins):
                steps[0] += 1
                ins.then_inc(dve_step, 1)
                dve.wait_ge(dve_step, steps[0])

            v = nc.vector
            for s in (*g_free, *f_free):
                dve.sem_inc(s, 1)
            dve.wait_ge(consts_set, 9)
            v.tensor_scalar(ident[:, :], iota_f[:, :], iota_p[:, 0:1], None, ALU.is_equal).then_inc(ident_set, 1)
            dve.wait_ge(ident_set, 1)
            for h in range(HEADS):
                link(v.tensor_copy(spread[:, :, h], ident[0:GT, 0:GT]))

            dve.wait_ge(keys_in, 32)
            link(v.tensor_copy(keys[0:125, :], keys_i[0:125, :]))
            link(v.tensor_tensor(scrap[0:125, 0:80], keys[0:125, 0:80], keys[0:125, 1:81], ALU.is_gt))
            link(v.tensor_reduce(stat[0:125, 0:1], scrap[0:125, 0:80], AX_X, ALU.add))
            for c in range(1, CHUNKS):
                link(v.tensor_scalar(scrap[0:125, 0:80], keys[0:125, 0:80], float(c * P), None, ALU.is_lt,
                                     ALU.add, accum_out=stat[0:125, c:c + 1]))
            link(v.tensor_copy(scrap[0:125, 0:5], stat[0:125, :]))
            v.tensor_copy(stat[0:125, :], scrap[0:125, 0:5]).then_inc(stats_ready, 1)
            dve.wait_ge(counts_ready, 1)
            link(v.tensor_copy(cnt[:, :], ps[:, CNT_PS:CNT_PS + 5]))
            v.tensor_copy(flag_i[:, :], cnt[:, 0:1]).then_inc(flag_ready, 1)

            link(v.memset(off[:, 0:1], 0.0))
            link(v.memset(off[:, 5:6], float(EDGES)))
            link(v.tensor_copy(off[:, 1:5], cnt[:, 1:5]))
            link(v.tensor_tensor(seg_n[:, :], off[:, 1:6], off[:, 0:5], ALU.subtract))
            for c in range(CHUNKS):
                link(v.tensor_scalar(scrap[:, 0:80], iota_128k[:, :], seg_n[:, c:c + 1], None, ALU.is_lt,
                                     ALU.add, accum_out=seg_t[:, c:c + 1]))
            link(v.memset(tile0[:, 0:1], 0.0))
            link(v.tensor_tensor_scan(tile0[:, 1:6], ones[:, 0:5], seg_t[:, :], 0.0, ALU.mult, ALU.add))
            link(v.tensor_copy(off_i[:, :], off[:, :]))
            link(v.tensor_copy(tile0_i[:, :], tile0[:, :]))
            link(v.tensor_scalar(ct[:, :], iota_t[:, :], tile0[:, 1:2], None, ALU.is_ge))
            for c in range(2, CHUNKS):
                link(v.scalar_tensor_tensor(out=ct[:, :], in0=iota_t[:, :], scalar=tile0[:, c:c + 1],
                                            in1=ct[:, :], op0=ALU.is_ge, op1=ALU.add))
            link(v.tensor_scalar(node_no[:, :], ct[:, :], float(P), iota_p[:, 0:1], ALU.mult, ALU.add))
            v.tensor_copy(ct_i[:, :], ct[:, :]).then_inc(tile_tables, 1)

            dve.wait_ge(flag_ready, 1)
            unsorted = dve.value_load(flag_i[0:1, 0:1], min_val=0, max_val=EDGES)
            with dve.If(unsorted > 0):
                dve.wait_ge(rank_cols, 32)
                dve.wait_ge(rank_iota, 2)
                v.tensor_copy(rk_kcol, rk_col_i[:, 1, :]).then_inc(rank_iota, 1)
                dve.wait_ge(rank_iota, 3)
                v.scalar_tensor_tensor(out=rk_kcol, in0=rk_kcol, scalar=SORT_SHIFT, in1=rk_eno,
                                       op0=ALU.mult, op1=ALU.add).then_inc(rank_iota, 1)
                for b in range(RBLOCKS):
                    dve.wait_ge(rank_blk, 16 * (b + 1))
                    dve.wait_ge(rank_iota, 4 + 3 * b)
                    v.tensor_copy(rk_key, rk_int).then_inc(rank_iota, 1)
                    dve.wait_ge(rank_iota, 5 + 3 * b)
                    v.scalar_tensor_tensor(out=rk_key, in0=rk_key, scalar=SORT_SHIFT, in1=rk_iota,
                                           op0=ALU.mult, op1=ALU.add).then_inc(rank_iota, 1)
                    dve.wait_ge(rank_iota, 6 + 3 * b)
                    with dve.Fori(0, ETILES) as t:
                        v.tensor_scalar(rk_out, rk_key, rk_kcol[:, bass.ds(t, 1)], None, ALU.is_lt, ALU.add,
                                        accum_out=rk_cnt[:, bass.ds(t + b * ETILES, 1)]).then_inc(rank_tile, 1)
                        dve.wait_ge(rank_tile, t + (1 + b * ETILES))
                    v.tensor_scalar(rk_kcol, rk_kcol, float(-RB), None, ALU.add).then_inc(rank_iota, 1)
                    dve.wait_ge(rank_iota, 7 + 3 * b)
                    v.tensor_copy(scrap[0:1, 0:1], rk_kcol[0:1, 0:1]).then_inc(rank_used, 1)
                dve.wait_ge(rank_used, RBLOCKS)
                v.tensor_reduce(rk_pos, rk_cnt.rearrange("p (b t) -> p t b", b=RBLOCKS), AX_X, ALU.add
                                ).then_inc(rank_iota, 1)
                dve.wait_ge(rank_iota, 5 + 3 * RBLOCKS)
                v.tensor_copy(rk_pos_i[:, 0, :], rk_pos).then_inc(rank_iota, 1)
                v.tensor_scalar(rk_pos_i[:, 1, :], rk_pos, float(STAGE), None, ALU.add).then_inc(ranked, 1)
            link(v.memset(cont[:, 0:1], 0.0))

            def evacuate(l, g):
                c, b = g // 2, g % 2
                bias = (bias_s, bias_d)[b]
                if g == 0:
                    dve.wait_ge(bias_in, 32 * (l + 1))
                    dve.wait_ge(attn_in, 16 * (l + 1))
                dve.wait_ge(proj_ready[b], CHUNKS * l + c + 1)
                if b == 0 and (c > 0 or l > 0):
                    dve.wait_ge(table_stored, 16 * (CHUNKS * l + c))
                if b == 1 and (c > 0 or l > 0):
                    dve.wait_ge(fd_ready, 2 * (CHUNKS * l + c))
                v.tensor_tensor(stage_f[:, b, 0:DIM].rearrange("p (a n) -> p a n", a=2),
                                ps[:, b * 1024:(b + 1) * 1024].rearrange("p (a n) -> p a n", a=2)[:, :, 0:HALF],
                                bias[:, :].rearrange("p (a n) -> p a n", a=2), ALU.add).then_inc(proj_free[b], 1)
                dve.wait_ge(proj_free[b], CHUNKS * l + c + 1)
                link(v.tensor_tensor(prod[:, :], stage_f[:, b, 0:DIM], attn[:, :], ALU.mult))
                last = v.tensor_reduce(stage_f[:, b, DIM:ROW], prod[:, :].rearrange("p (h d) -> p h d", h=HEADS),
                                       AX_X, ALU.add)
                last.then_inc(row_ready[b], 1)
                if b == 1:
                    for k in range(2):
                        dve.wait_ge(fd_part, 2 * (CHUNKS * l + c) + k + 1)
                        if k == 0:
                            v.tensor_tensor(stage_f[:, 1, :], stage_f[:, 1, :], fd3[:, c, 0, :], ALU.subtract
                                            ).then_inc(row_ready[1], 1)
                        else:
                            v.tensor_tensor(fd3[:, c, 2, :], stage_f[:, 1, :], fd3[:, c, 1, :], ALU.subtract
                                            ).then_inc(fd_ready, 2)

            def slot_tables():
                dve.wait_ge(rows_in, 32)
                v.tensor_copy(rows_f[:, :, :], rows_i[:, :, :]).then_inc(rows_conv, 1)
                dve.wait_ge(e16_in, 16)
                v.tensor_copy(e16, e16_i).then_inc(e16_conv, 1)
                dve.wait_ge(rows_turned, 1)
                v.tensor_copy(src_i[:, :], ps[:, SRC_PS:SRC_PS + TPAD]).then_inc(src_ready, 1)
                link(v.scalar_tensor_tensor(out=dst_rel[:, :], in0=ct[:, :], scalar=float(-P),
                                            in1=ps[:, DST_PS:DST_PS + TPAD], op0=ALU.mult, op1=ALU.add))
                dve.wait_ge(dstbc_in, 16)
                v.tensor_tensor(ohT[:, :, :], dst_bc,
                                node_no[:, 0:TILES].rearrange("p (t o) -> p t o", o=1).to_broadcast([P, TILES, P]),
                                ALU.is_equal).then_inc(ohT_ready, 1)
                dve.wait_ge(dst_spread, 1)
                for a in range(2):
                    link(v.tensor_copy(dst_ht[:, 3 * a:3 * a + 3, :],
                                       ps[:, E_PS[a]:E_PS[a] + HALF].rearrange("p (g e) -> p g e", g=3)))
                d = dst_ht
                link(v.memset(pen[:, 0, :, 0:1], 1.0))
                link(v.memset(pen[:, 1, :, P - 1:P], 1.0))
                link(v.tensor_tensor(pen[:, 0, :, 1:P], d[:, :, 1:P], d[:, :, 0:P - 1], ALU.not_equal))
                link(v.tensor_tensor(pen[:, 1, :, 0:P - 1], d[:, :, 1:P], d[:, :, 0:P - 1], ALU.not_equal))
                link(v.tensor_tensor(pen[:, 2, :, :], d[:, :, :], d[:, :, 0:1].to_broadcast([P, GROUPS, P]),
                                     ALU.not_equal))
                link(v.tensor_tensor(pen[:, 3, :, :], d[:, :, :], d[:, :, P - 1:P].to_broadcast([P, GROUPS, P]),
                                     ALU.not_equal))
                flat = pen[:, :, :, :].rearrange("p a g e -> p (a g e)")
                link(v.tensor_scalar(flat, flat, NO, None, ALU.mult))
                dve.wait_ge(ends_in, 32)
                link(v.tensor_copy(ends[:, :, :], ends_i[:, :, :]))
                n = TPAD
                link(v.tensor_tensor(single[:, :], ends[:, 0, :], ends[:, 1, :], ALU.is_equal))
                link(v.tensor_tensor(cont[:, 1:n], ends[:, 0, 1:n], ends[:, 1, 0:n - 1], ALU.is_equal))
                link(v.tensor_tensor(tmp_row[:, 1:n], ct[0:1, 1:n], ct[0:1, 0:n - 1], ALU.is_equal))
                link(v.tensor_tensor(cont[:, 1:n], cont[:, 1:n], tmp_row[:, 1:n], ALU.mult))
                cp = chain_pen
                link(v.memset(cp[:, :, :], 0.0))
                link(v.tensor_tensor(cp[:, 0, 1:n], single[:, 0:n - 1], cont[:, 1:n], ALU.mult))
                link(v.tensor_copy(cp[:, 1, 1:n], cont[:, 1:n]))
                link(v.tensor_tensor(cp[:, 2, 0:n - 1], single[:, 1:n], cont[:, 1:n], ALU.mult))
                link(v.tensor_copy(cp[:, 3, 0:n - 1], cont[:, 1:n]))
                link(v.tensor_scalar(cp[:, :, :], cp[:, :, :], -NO, NO, ALU.mult, ALU.add))
                for a in range(2):
                    link(v.tensor_copy(chain_a[:, a, :, :], cp[:, 2 * a:2 * a + 1, :].to_broadcast([1, HEADS, n])))

            def edge_logits(l):
                at = attn

                def turn(i, first, us=UN):
                    for u in range(us):
                        b = u % 2
                        n2 = i * 2 + (u // 2 + 2 * TURNS * l)
                        t = i * UN + u
                        dve.wait_ge(gathered[u], i * 16 + (16 + 16 * TURNS * 2 * l))
                        dve.wait_ge(f_ready[b], n2 + 1)
                        if not (first and l == 0 and u < 2):
                            dve.wait_ge(lin_kept[b], n2)
                        f0 = ps[:, b * 1024:b * 1024 + HALF]
                        f1 = ps[:, b * 1024 + 512:b * 1024 + 512 + HALF + HEADS]
                        v.tensor_tensor(sums[:, b, :], gat[:, u, HALF:ROW], f1, ALU.add).then_inc(sum_ready[b], 1)
                        if not (first and u < 2):
                            if l == 0:
                                dve.wait_ge(reduced, t - 1)
                            elif u < 2:
                                dve.wait_ge(g_free[u + 2], i + (1 + 2 * TURNS))
                            else:
                                dve.wait_ge(g_free[u - 2], i + (2 + 2 * TURNS))
                        acc = dict(accum_out=relu_sum[:, bass.ds(t, 1), 0:1].rearrange("p a o -> p (a o)")) if l else {}
                        v.scalar_tensor_tensor(out=prods[:, b, 0:HALF], in0=f0, scalar=0.0, in1=at[:, 0:HALF],
                                               op0=ALU.max, op1=ALU.mult, **acc).then_inc(f_free[b], 1)
                        dve.wait_ge(sum_ready[b], n2 + 1)
                        acc = dict(accum_out=relu_sum[:, bass.ds(t, 1), 1:2].rearrange("p a o -> p (a o)")) if l else {}
                        v.scalar_tensor_tensor(out=prods[:, b, HALF:DIM], in0=sums[:, b, 0:HALF], scalar=0.0,
                                               in1=at[:, HALF:DIM], op0=ALU.max, op1=ALU.mult, **acc
                                               ).then_inc(g_free[u], 1)
                        if l == 0 and not (first and u == 0):
                            reduce_tile(t - 1, (u - 1) % UN, i if u else i - 1)

                def reduce_tile(t, u, i):
                    b = u % 2
                    dve.wait_ge(g_free[u], i + 2)
                    v.tensor_reduce(relu_sum[:, bass.ds(t, 1), :].rearrange("p a h -> p (a h)"),
                                    prods[:, b, :].rearrange("p (h d) -> p h d", h=HEADS), AX_X, ALU.add
                                    ).then_inc(reduced, 1)

                turn(0, True)
                with dve.Fori(1, TURNS) as i:
                    turn(i, False)
                if l == 0:
                    reduce_tile(TILES - 1, UN - 1, TURNS - 1)

            def softmax(l):
                for b in range(2):
                    dve.wait_ge(lin_kept[b], 2 * TURNS * (l + 1))
                if l == 0:
                    dve.wait_ge(reduced, TILES)
                    v.scalar_tensor_tensor(out=logits[:, :, :], in0=lin[:, :, :], scalar=SLOPE / (1.0 - SLOPE),
                                           in1=relu_sum[:, :, :], op0=ALU.mult, op1=ALU.add
                                           ).then_inc(logits_ready, 1)
                else:
                    for u in range(UN):
                        dve.wait_ge(g_free[u], TURNS * 3 + 1)
                    link(v.tensor_reduce(scrap[:, 0:TPAD], lin[:, :, :], AX_X, ALU.add))
                    link(v.scalar_tensor_tensor(
                        out=scrap[:, 0:TPAD], in0=scrap[:, 0:TPAD], scalar=SLOPE / (1.0 - SLOPE),
                        in1=relu_sum[:, :, 0], op0=ALU.mult, op1=ALU.add))
                    v.tensor_tensor(logits[:, :, 0], scrap[:, 0:TPAD], relu_sum[:, :, 1], ALU.add
                                    ).then_inc(logits_ready, 1)
                flat = lambda a: a.rearrange("p g e -> p (g e)")
                dve.wait_ge(lt_ready, l + 1)
                link(v.tensor_tensor_scan(flat(mx), flat(pen[:, 0, :, :]), flat(lt), NO, ALU.add, ALU.max))
                v.tensor_tensor_scan(flat(mx2)[:, ::-1], flat(pen[:, 1, :, :])[:, ::-1], flat(mx)[:, ::-1],
                                     NO, ALU.add, ALU.max).then_inc(tile_max, 1)
                dve.wait_ge(ends_turned, l + 1)
                n = TPAD
                hm = lambda r, a: r[0:1, a, :].rearrange("p (h t) -> p h t", h=HEADS)
                for a in range(2):
                    link(v.tensor_copy(hm(mrow, a), ps[0:1, 1024 * (a + 1):1024 * (a + 1) + DIM]
                                       .rearrange("p (t h) -> p h t", h=HEADS)))
                link(v.memset(brow[0:1, :, :], NO))
                link(v.tensor_tensor(hm(brow, 0)[:, :, 1:n], hm(mrow, 0)[:, :, 0:n - 1],
                                     chain_pen[:, 1:2, 1:n].to_broadcast([1, HEADS, n - 1]), ALU.add))
                link(v.tensor_tensor(hm(brow, 1)[:, :, 0:n - 1], hm(mrow, 1)[:, :, 1:n],
                                     chain_pen[:, 3:4, 0:n - 1].to_broadcast([1, HEADS, n - 1]), ALU.add))
                ca = chain_a[:, :, :, :].rearrange("p a h t -> p a (h t)")
                link(v.tensor_tensor_scan(srow[0:1, 0, :], ca[:, 0, :], brow[0:1, 0, :], NO, ALU.add, ALU.max))
                link(v.tensor_tensor_scan(srow[0:1, 1, ::-1], ca[:, 1, ::-1], brow[0:1, 1, ::-1],
                                          NO, ALU.add, ALU.max))
                for a in range(2):
                    v.tensor_copy(brow[0:1, a, :].rearrange("p (t h) -> p h t", h=HEADS), hm(srow, a)
                                  ).then_inc(chain_ready, 1)
                dve.wait_ge(chain_spread, l + 1)
                link(v.tensor_copy(carry, ps[:, 3072:3072 + 2 * GROUPS]))
                for a, (i0, o) in enumerate(((mx2, mx), (mx, mx2))):
                    for g in range(GROUPS):
                        link(v.scalar_tensor_tensor(
                            out=o[:, g, :], in0=pen[:, 2 + a, g, :], scalar=carry[:, a * GROUPS + g:a * GROUPS + g + 1],
                            in1=i0[:, g, :], op0=ALU.add, op1=ALU.max))
                v.tensor_tensor(lt, lt, mx2, ALU.subtract).then_inc(shifted, 1)

            def aggregation_inputs(l):
                dve.wait_ge(ex_ready, l + 1)
                with dve.Fori(0, TURNS) as i:
                    for u in range(UN):
                        b = u % 2
                        t = i * UN + u
                        dve.wait_ge(agg_free[b], i * 2 + (u // 2 + 1 + 2 * TURNS * l))
                        if l == 0:
                            v.tensor_scalar(onehot[:, b, :], iota_f[:, :], dst_rel[:, bass.ds(t, 1)], None,
                                            ALU.is_equal)
                            dve.wait_ge(gathered[u], i * 16 + (16 + 16 * TURNS))
                            v.tensor_tensor(prods[:, b, :].rearrange("p (h d) -> p h d", h=HEADS),
                                            gat[:, u, 0:DIM].rearrange("p (h d) -> p h d", h=HEADS),
                                            ex[:, bass.ds(t, 1), :].rearrange("p a h -> p h a")
                                            .to_broadcast([P, HEADS, HD]), ALU.mult).then_inc(agg_in[b], 1)
                        else:
                            v.tensor_scalar(onehot[:, b, :], iota_f[:, :], dst_rel[:, bass.ds(t, 1)],
                                            ex[:, bass.ds(t, 1), 0:1].rearrange("p a o -> p (a o)"),
                                            ALU.is_equal, ALU.mult).then_inc(agg_in[b], 1)

            def moments(c):
                for a in range(2):
                    link(v.bn_stats(bn6[:, c, a, :], v_sb[:, c, a * HALF:(a + 1) * HALF]))
                link(v.bn_aggr(mv[:, c, :], bn6[:, c, :, :].rearrange("p a s -> p (a s)")))

            def inverse_deviation(n):
                v.tensor_scalar(var_e[:, :], mv[:, :, 1], EPS, None, ALU.add).then_inc(var_ready, 1)
                dve.wait_ge(root_ready, n)
                link(v.reciprocal(rstd[:, :], root[:, :]))
                link(v.tensor_tensor(nt1[:, :], rstd[:, :], rstd[:, :], ALU.mult))
                link(v.tensor_tensor(nt1[:, :], nt1[:, :], var_e[:, :], ALU.mult))
                link(v.tensor_scalar(nt1[:, :], nt1[:, :], -0.5, 1.5, ALU.mult, ALU.add))
                link(v.tensor_tensor(rstd[:, :], rstd[:, :], nt1[:, :], ALU.mult))

            def nodes(l):
                dve.wait_ge(agg_done, l + 1)
                link(v.tensor_scalar(rden[:, :], ps[:, DEN:DEN + CHUNKS * HEADS], TINY, None, ALU.max))
                link(v.reciprocal(rden[:, :], rden[:, :]))
                for c in range(CHUNKS):
                    v.tensor_tensor(v_sb[:, c, :].rearrange("p (h d) -> p h d", h=HEADS),
                                    ps[:, c * DIM:(c + 1) * DIM].rearrange("p (h d) -> p h d", h=HEADS),
                                    rden[:, c * HEADS:(c + 1) * HEADS].rearrange("p (h o) -> p h o", o=1)
                                    .to_broadcast([P, HEADS, HD]), ALU.mult).then_inc(normed, 1)
                    dve.wait_ge(normed, CHUNKS * l + c + 1)
                    v.tensor_scalar(neg[:, c % 2, :], v_sb[:, c, :], 0.0, None, ALU.min).then_inc(neg_ready, 1)
                    dve.wait_ge(neg_exp, CHUNKS * l + c + 1)
                    dve.wait_ge(pos_ready, CHUNKS * l + c + 1)
                    v.tensor_tensor(v_sb[:, c, :], neg[:, c % 2, :], posm[:, c % 2, :], ALU.add).then_inc(elu_used, 1)
                    dve.wait_ge(elu_used, CHUNKS * l + c + 1)
                    if l == 0:
                        link(v.tensor_tensor(v_sb[:, c, :], v_sb[:, c, :], x_sb[:, c, :], ALU.add))
                    moments(c)
                inverse_deviation(l + 1)
                dve.wait_ge(norm_in, 32 * (l + 1))
                for c in range(CHUNKS):
                    link(v.tensor_scalar(v_sb[:, c, :], v_sb[:, c, :], mv[:, c, 0:1], rstd[:, c:c + 1],
                                         ALU.subtract, ALU.mult))
                    link(v.tensor_tensor(v_sb[:, c, :], v_sb[:, c, :], ln_w[:, :], ALU.mult))
                    last = v.tensor_tensor(v_sb[:, c, :], v_sb[:, c, :], ln_b[:, :], ALU.add)
                    if l == 0:
                        last.then_inc(h_ready, 1)
                    else:
                        link(last)
                        link(v.tensor_tensor(v_sb[:, c, :], v_sb[:, c, :], x_sb[:, c, :], ALU.add))
                        moments(c)
                if l == 1:
                    inverse_deviation(3)
                    for c in range(CHUNKS):
                        v.tensor_scalar(v_sb[:, c, :], v_sb[:, c, :], mv[:, c, 0:1], rstd[:, c:c + 1],
                                        ALU.subtract, ALU.mult).then_inc(out_ready, 1)

            for g in range(6):
                evacuate(0, g)
            slot_tables()
            for g in range(6, 2 * CHUNKS):
                evacuate(0, g)
            for l in range(2):
                if l == 1:
                    for g in range(2 * CHUNKS):
                        evacuate(1, g)
                edge_logits(l)
                softmax(l)
                aggregation_inputs(l)
                nodes(l)


_INS = ['x', 'src', 'dst', 'L0_gnn_W1s', 'L0_gnn_b1s', 'L0_gnn_W1d', 'L0_gnn_b1d', 'L0_gnn_attn1',
        'L0_gnn_ln1_w', 'L0_gnn_ln1_b', 'L0_gnn_Wos', 'L0_gnn_bos', 'L0_gnn_Wod', 'L0_gnn_bod',
        'L0_gnn_attno', 'L0_gnn_lno_w', 'L0_gnn_lno_b']
_OUTS = [((NODES, DIM), 'float32')]


def kernel(**inputs):
    import numpy as _np
    import concourse.bacc as _bacc
    from concourse import mybir as _mybir
    from concourse.bass_utils import run_bass_kernel_spmd as _run

    nc = _bacc.Bacc("TRN2", target_bir_lowering=False, num_devices=1)
    arrays, args = {}, []
    for name in _INS:
        a = _np.ascontiguousarray(inputs[name])
        arrays[f"in_{name}_dram"] = a
        args.append(nc.dram_tensor(f"in_{name}_dram", a.shape, _mybir.dt.from_np(a.dtype), kind="ExternalInput").ap())
    for i, (shape, dtype) in enumerate(_OUTS):
        dt = _mybir.dt.from_np(_np.dtype(dtype))
        args.append(nc.dram_tensor(f"out_{i}_dram", shape, dt, kind="ExternalOutput").ap())
    gat_kernel(nc, *args)
    r = _run(nc, [arrays], core_ids=[0])
    got = tuple(r.results[0][f"out_{i}_dram"] for i in range(len(_OUTS)))
    return got[0]
```

```python
from contextlib import ExitStack

import concourse.bass as bass
from concourse import mybir

ALU = mybir.AluOpType
ACT = mybir.ActivationFunctionType
AX_X = mybir.AxisListType.X
F32 = mybir.dt.float32
BF16 = mybir.dt.bfloat16
I32 = mybir.dt.int32

P = 128
NODES, EDGES, DIM, HEADS = 625, 10000, 768, 8
HD = DIM // HEADS
HALF = DIM // 2
KC = DIM // P
CHUNKS = -(-NODES // P)
LAST = NODES - (CHUNKS - 1) * P
TILES = 84
GROUPS = 6
GT = 16
TPAD = GROUPS * GT
ROW = DIM + HEADS
UN = 6
TURNS = TILES // UN
FB = 3
SPLIT = (384, 320)
EB = 3
DH = 2
QW = 256
DEN = CHUNKS * DIM
SLOTS = TPAD * P
STAGE = EDGES + SLOTS
PAD_DST = 1000.0
NO = -1.0e30
EPS = 1e-5
SLOPE = 0.2
SORT_SHIFT = 16384.0
ETILES = -(-EDGES // P)
RB = 1264
RBLOCKS = ETILES * P // RB
TINY = 1e-30


def gat_kernel(nc, x, src, dst, w1s, b1s, w1d, b1d, attn1, ln1w, ln1b,
               wos, bos, wod, bod, attno, lnow, lnob, out):
    staged = nc.dram_tensor("staged_edges", [2, STAGE], I32, kind="Internal").ap()
    runs = nc.dram_tensor("chunk_runs", [CHUNKS, 2, SLOTS], I32, kind="Internal").ap()
    rel_rows = nc.dram_tensor("relative_dst", [TPAD, P], BF16, kind="Internal").ap()
    tables = [nc.dram_tensor(f"fs_table{l}", [NODES, ROW], F32, kind="Internal").ap() for l in range(2)]

    with ExitStack() as ctx:
        def sb(name, shape, dt):
            return ctx.enter_context(nc.sbuf_tensor(name, shape, dt))

        def sem(name):
            return ctx.enter_context(nc.semaphore(name))

        x_sb = sb("x_sb", [P, CHUNKS, DIM], F32)
        actT = sb("actT", [P, KC, CHUNKS * P], F32)
        w_s = sb("w_s", [P, KC, DIM], F32)
        w_d = sb("w_d", [P, KC, DIM], F32)
        attn = sb("attn", [P, DIM], F32)
        vec = [sb(f"vec{i}", [P, DIM], F32) for i in range(2)]
        bias_s, bias_d = vec
        ln_w, ln_b = vec
        fd3 = sb("fd3", [P, CHUNKS, 3, ROW], BF16)
        ohT = sb("ohT", [P, TILES, P], BF16)
        arena = sb("arena", [P, TILES * P], F32)
        ident = sb("ident", [P, P], F32)
        ones = sb("ones", [P, P], F32)
        iota_f = sb("iota_f", [P, P], F32)
        iota_t = sb("iota_t", [P, TPAD], F32)
        iota_128k = sb("iota_128k", [P, 80], F32)
        iota_p = sb("iota_p", [P, 1], F32)
        zero_w = sb("zero_w", [P, P], BF16)
        zero_m = sb("zero_m", [P, 512], BF16)
        pads = sb("pads", [P, 2, SLOTS // P], I32)
        keys_i = sb("keys_i", [P, 81], I32)
        keys = sb("keys", [P, 81], F32)
        scrap = sb("scrap", [P, 128], F32)
        stat = sb("stat", [P, 5], F32)
        flag_i = sb("flag_i", [P, 1], I32)
        off = sb("off", [P, 6], F32)
        seg_n = sb("seg_n", [P, 5], F32)
        seg_t = sb("seg_t", [P, 5], F32)
        run_step = sb("run_step", [P, 5], F32)
        tile_p = sb("tile_p", [P, 10], F32)
        run_base = sb("run_base", [P, 1], F32)
        chunk_p = sb("chunk_p", [P, 1], F32)
        run_idx = sb("run_idx", [P, 2], I32)
        tile0 = sb("tile0", [P, 6], F32)
        off_i = sb("off_i", [P, 6], I32)
        ct = sb("ct", [1, TPAD], F32)
        ct_i = sb("ct_i", [1, TPAD], I32)
        rows_i = sb("rows_i", [TPAD, 2, P], I32)
        rows_f = sb("rows_f", [TPAD, 2, P], F32)
        rel_b = sb("rel_b", [TPAD, P], BF16)
        src_i = sb("src_i", [P, TPAD], I32)
        dst_rel = sb("dst_rel", [P, TPAD], F32)
        pen = sb("pen", [P, 4, GROUPS, P], BF16)
        ends = sb("ends", [1, 2, TPAD], F32)
        single = sb("single", [1, TPAD], F32)
        cont = sb("cont", [1, TPAD], F32)
        tmp_row = sb("tmp_row", [1, TPAD], F32)
        chain_pen = sb("chain_pen", [1, 4, TPAD], F32)
        chain_a = sb("chain_a", [1, 2, HEADS, TPAD], BF16)
        relu_sum = sb("relu_sum", [P, TPAD, HEADS], F32)
        lin = sb("lin", [P, TPAD, HEADS], F32)
        logits = sb("logits", [P, TPAD, HEADS], F32)
        ex = sb("ex", [P, TPAD, HEADS], F32)
        idx_now = sb("idx_now", [P, UN], I32)
        rden = sb("rden", [P, CHUNKS * HEADS], F32)
        bn6 = sb("bn6", [P, CHUNKS, 2, 6], F32)
        mv = sb("mv", [P, CHUNKS, 2], F32)
        var_e = sb("var_e", [P, CHUNKS], F32)
        root = sb("root", [P, CHUNKS], F32)
        rstd = sb("rstd", [P, CHUNKS], F32)
        nt1 = sb("nt1", [P, CHUNKS], F32)

        ps = ctx.enter_context(nc.psum_tensor("ps", [P, 4096], F32))

        def part(at, *shape):
            n = 1
            for s in shape:
                n *= s
            v = arena[:, at:at + n]
            if len(shape) == 2:
                return v.rearrange("p (a b) -> p a b", a=shape[0])
            if len(shape) == 3:
                return v.rearrange("p (a b c) -> p a b c", a=shape[0], b=shape[1])
            return v

        dst_bc = arena[:, 0:TILES * P // 2].bitcast(BF16)
        at_prep = 6400
        spread = part(at_prep, TPAD, HEADS)[0:TPAD]
        junk = part(at_prep + DIM, 10, 80)
        dst_ht = part(at_prep + DIM + 800, GROUPS, P)
        stage_f = sb("stage_f", [P, 2, ROW], F32)
        prod = sb("prod", [P, DIM], F32)
        gat = part(0, UN, ROW)
        prods = part(UN * ROW, 2, DIM)
        onehot = part(UN * ROW + 2 * DIM, 2, P)
        at_sm = UN * ROW + 2 * DIM + 2 * P
        lt = part(at_sm, GROUPS, P)
        mx = part(at_sm + DIM, GROUPS, P)
        mx2 = part(at_sm + 2 * DIM, GROUPS, P)
        mrow = part(at_sm + 3 * DIM, 2, DIM)
        brow = prods
        srow = mrow
        carry = part(at_sm + 5 * DIM, 2 * GROUPS)
        v_sb = part(0, CHUNKS, DIM)
        ev = part(CHUNKS * DIM, EB, DIM)
        posm = part((CHUNKS + EB) * DIM, EB, DIM)
        rk_int = arena[:, 0:RB].bitcast(I32)
        rk_key = arena[:, RB:2 * RB]
        rk_iota = arena[:, 2 * RB:3 * RB]
        rk_out = arena[:, 3 * RB:4 * RB]
        rk_cnt = arena[:, 4 * RB:4 * RB + RBLOCKS * ETILES]
        at_rk = 4 * RB + RBLOCKS * ETILES
        rk_col_i = arena[:, at_rk:at_rk + 2 * ETILES].bitcast(I32).rearrange("p (a t) -> p a t", a=2)
        rk_eno = arena[:, at_rk + 2 * ETILES:at_rk + 3 * ETILES]
        rk_kcol = arena[:, at_rk + 3 * ETILES:at_rk + 4 * ETILES]
        rk_pos = arena[:, at_rk + 4 * ETILES:at_rk + 5 * ETILES]
        rk_pos_i = arena[:, at_rk + 5 * ETILES:at_rk + 7 * ETILES].bitcast(I32).rearrange("p (a t) -> p a t", a=2)
        rk_idx = arena[:, at_rk + 7 * ETILES:at_rk + 7 * ETILES + 2].bitcast(I32)
        rk_val = arena[:, at_rk + 7 * ETILES + 2:at_rk + 7 * ETILES + 4].bitcast(I32)
        assert at_rk + 7 * ETILES + 4 <= at_prep

        pads_set = sem("pads_set")
        consts_set = sem("consts_set")
        ident_set = sem("ident_set")
        staged_in = sem("staged_in")
        keys_in = sem("keys_in")
        stats_ready = sem("stats_ready")
        counts_ready = sem("counts_ready")
        flag_ready = sem("flag_ready")
        rank_cols = sem("rank_cols")
        rank_blk = sem("rank_blk")
        rank_used = sem("rank_used")
        rank_iota = sem("rank_iota")
        ranked = sem("ranked")
        rank_tile = sem("rank_tile")
        rank_copy = sem("rank_copy")
        rank_out = sem("rank_out")
        edges_sorted = sem("edges_sorted")
        run_starts = sem("run_starts")
        tile_tables = sem("tile_tables")
        runs_made = sem("runs_made")
        rel_stored = sem("rel_stored")
        rows_in = sem("rows_in")
        dstbc_in = sem("dstbc_in")
        rows_conv = sem("rows_conv")
        rows_turned = sem("rows_turned")
        src_ready = sem("src_ready")
        dst_spread = sem("dst_spread")
        spread_copied = sem("spread_copied")
        ohT_ready = sem("ohT_ready")
        x_in = [sem(f"x_in{c}") for c in range(CHUNKS)]
        ws_in = [sem(f"ws_in{a}") for a in range(2)]
        wd_in = sem("wd_in")
        bias_in = sem("bias_in")
        norm_in = sem("norm_in")
        attn_in = sem("attn_in")
        turned = [sem(f"turned{b}") for b in range(2)]
        turn_copied = [sem(f"turn_copied{b}") for b in range(2)]
        proj_ready = [sem(f"proj_ready{b}") for b in range(2)]
        proj_free = [sem(f"proj_free{b}") for b in range(2)]
        row_ready = [sem(f"row_ready{b}") for b in range(2)]
        table_stored = sem("table_stored")
        fd_ready = sem("fd_ready")
        fd_part = sem("fd_part")
        gathered = [sem(f"gathered{u}") for u in range(UN)]
        g_free = [sem(f"g_free{u}") for u in range(UN)]
        idx_set = sem("idx_set")
        f_ready = [sem(f"f_ready{b}") for b in range(FB)]
        f_free = [sem(f"f_free{b}") for b in range(FB)]
        sum_ready = sem("sum_ready")
        heads_dve = sem("heads_dve")
        heads_act = sem("heads_act")
        logits_ready = sem("logits_ready")
        logits_turned = sem("logits_turned")
        lt_ready = sem("lt_ready")
        tile_max = sem("tile_max")
        ends_turned = sem("ends_turned")
        chain_ready = sem("chain_ready")
        chain_spread = sem("chain_spread")
        shifted = sem("shifted")
        exped = sem("exped")
        ex_turned = sem("ex_turned")
        ex_ready = sem("ex_ready")
        zeros_set = sem("zeros_set")
        agg_in = [sem(f"agg_in{b}") for b in range(2)]
        agg_free = [sem(f"agg_free{b}") for b in range(2)]
        agg_done = sem("agg_done")
        normed = sem("normed")
        v_exp = sem("v_exp")
        pos_ready = sem("pos_ready")
        elu_used = sem("elu_used")
        xb_ready = sem("xb_ready")
        var_ready = sem("var_ready")
        root_ready = sem("root_ready")
        h_ready = sem("h_ready")
        out_ready = sem("out_ready")
        out_stored = sem("out_stored")
        dve_step = sem("dve_step")

        TURN_PS = [2048, 2560]
        SPREAD_PS = [3584, 3072]
        SRC_PS, DST_PS, ENDS_PS, CNT_PS = 3072, 3072 + TPAD, 3072 + 2 * TPAD, 3984

        block = ctx.enter_context(nc.Block())

        @block.sync
        def _(sp):
            sp.wait_ge(pads_set, 3)
            sp.dma_start(keys_i[0:125, 0:80], dst.rearrange("(p n) -> p n", p=125)).then_inc(keys_in, 16)
            with nc.allow_non_contiguous_dma("the first key of the next partition"):
                sp.dma_start(keys_i[0:124, 80:81], dst[80:EDGES].rearrange("(p n) -> p n", p=124)[:, 0:1]
                             ).then_inc(keys_in, 16)
            for a, v in enumerate((src, dst)):
                sp.dma_start(staged[a, 0:EDGES].rearrange("(b n) -> b n", b=16),
                             v.rearrange("(b n) -> b n", b=16)).then_inc(staged_in, 16)
                sp.dma_start(staged[a, EDGES:STAGE].rearrange("(p n) -> p n", p=P),
                             pads[:, a, :]).then_inc(staged_in, 16)
            sp.wait_ge(staged_in, 64)
            sp.wait_ge(edges_sorted, 1)
            sp.wait_ge(run_starts, 1)
            for c in range(CHUNKS):
                frm = sp.value_load(off_i[0:1, c:c + 1], min_val=0, max_val=EDGES) if c else 0
                sp.dma_start(runs[c, :, :].rearrange("a (b n) -> a b n", b=16),
                             staged[:, bass.ds(frm, SLOTS)].rearrange("a (b n) -> a b n", b=16)
                             ).then_inc(runs_made, 16)
            sp.wait_ge(rows_conv, 3)
            sp.dma_start(rel_rows[:, :], rel_b[:, :]).then_inc(rel_stored, 16)
            sp.wait_ge(rel_stored, 16)
            sp.dma_start(dst_bc, rel_rows[0:TILES, :].rearrange("t e -> (t e)").partition_broadcast(P)
                         ).then_inc(dstbc_in, 16)
            for l in range(2):
                for c in range(CHUNKS):
                    n = P if c < CHUNKS - 1 else LAST
                    sp.wait_ge(row_ready[0], 5 * l + c + 1)
                    sp.dma_start(tables[l][c * P:c * P + n, :], stage_f[0:n, 0, :]).then_inc(table_stored, 16)
                if l == 0:
                    sp.wait_ge(fd_ready, 2 * CHUNKS)
                    for a in range(2):
                        at = slice(a * HALF, (a + 1) * HALF)
                        sp.dma_start(w_s[:, :, at], wos.rearrange("(k p) n -> p k n", p=P)[:, :, at]
                                     ).then_inc(ws_in[a], 16)
                    sp.dma_start(w_d[:, :, :], wod.rearrange("(k p) n -> p k n", p=P)).then_inc(wd_in, 16)
                    sp.dma_start(ln_w[:, :], ln1w.partition_broadcast(P)).then_inc(norm_in, 16)
                    sp.dma_start(ln_b[:, :], ln1b.partition_broadcast(P)).then_inc(norm_in, 16)
                    sp.wait_ge(logits_ready, 1)
                    sp.dma_start(attn[:, :], attno.rearrange("h d -> (h d)").partition_broadcast(P)
                                 ).then_inc(attn_in, 16)
                    sp.wait_ge(h_ready, CHUNKS)
                    sp.dma_start(bias_s[:, :], bos.partition_broadcast(P)).then_inc(bias_in, 16)
                    sp.dma_start(bias_d[:, :], bod.partition_broadcast(P)).then_inc(bias_in, 16)
                else:
                    sp.wait_ge(fd_ready, 4 * CHUNKS)
                    sp.dma_start(ln_w[:, :], lnow.partition_broadcast(P)).then_inc(norm_in, 16)
                    sp.dma_start(ln_b[:, :], lnob.partition_broadcast(P)).then_inc(norm_in, 16)
            for c in range(CHUNKS):
                n = P if c < CHUNKS - 1 else LAST
                sp.wait_ge(out_ready, c + 1)
                sp.dma_start(out[c * P:c * P + n, :], v_sb[0:n, c, :]).then_inc(out_stored, 16)
            sp.wait_ge(out_stored, 16 * CHUNKS)

        @block.gpsimd
        def _(pool):
            nc.gpsimd.memset(pads[:, 0, :], 0).then_inc(pads_set, 1)
            nc.gpsimd.memset(pads[:, 1, :], int(PAD_DST)).then_inc(pads_set, 1)
            nc.gpsimd.memset(keys_i[:, 80:81], int(PAD_DST)).then_inc(pads_set, 1)
            nc.gpsimd.memset(x_sb[:, CHUNKS - 1, :], 0.0).then_inc(pads_set, 1)
            for dstt, pattern, mult in ((iota_f[:, :], [[1, P]], 0), (iota_p[:, :], [[1, 1]], 1),
                                        (iota_t[:, :], [[1, TPAD]], 0), (iota_128k[:, :], [[P, 80]], 0)):
                nc.gpsimd.iota(dstt, pattern, base=0, channel_multiplier=mult,
                               allow_small_or_imprecise_dtypes=True).then_inc(consts_set, 1)
            nc.gpsimd.memset(ones[:, :], 1.0).then_inc(consts_set, 1)
            nc.gpsimd.memset(zero_w[:, :], 0.0).then_inc(consts_set, 1)
            nc.gpsimd.memset(zero_m[:, :], 0.0).then_inc(consts_set, 1)
            nc.gpsimd.memset(relu_sum[:, :, :], 0.0).then_inc(consts_set, 1)
            nc.gpsimd.memset(lin[:, :, :], 0.0).then_inc(consts_set, 1)

            pool.wait_ge(flag_ready, 1)
            unsorted = pool.value_load(flag_i[0:1, 0:1], min_val=0, max_val=EDGES)
            with pool.If(unsorted > 0):
                with nc.allow_non_contiguous_dma("edges to columns"):
                    for a in range(2):
                        pool.dma_start(rk_col_i[:, a, :], staged[a, 0:ETILES * P]
                                       .rearrange("(t p) -> p t", p=P)).then_inc(rank_cols, 16)
                nc.gpsimd.iota(rk_iota, [[1, RB]], base=0, channel_multiplier=0,
                               allow_small_or_imprecise_dtypes=True).then_inc(rank_iota, 1)
                nc.gpsimd.iota(rk_eno, [[P, ETILES]], base=0, channel_multiplier=1,
                               allow_small_or_imprecise_dtypes=True).then_inc(rank_iota, 1)
                for b in range(RBLOCKS):
                    if b > 0:
                        pool.wait_ge(rank_used, b)
                    pool.dma_start(rk_int, staged[1, b * RB:(b + 1) * RB].partition_broadcast(P)
                                   ).then_inc(rank_blk, 16)
                pool.wait_ge(ranked, 1)
                with pool.Fori(0, ETILES) as t:
                    for a in range(2):
                        nc.gpsimd.tensor_copy(rk_idx[:, a:a + 1], rk_pos_i[:, a, bass.ds(t, 1)]
                                              ).then_inc(rank_copy, 1)
                        nc.gpsimd.tensor_copy(rk_val[:, a:a + 1], rk_col_i[:, a, bass.ds(t, 1)]
                                              ).then_inc(rank_copy, 1)
                        pool.wait_ge(rank_copy, 4 * t + 2 * a + 2)
                        pool.nop(nofuse=True)
                        nc.gpsimd.indirect_dma_start(
                            out=staged.rearrange("a (n o) -> (a n) o", o=1),
                            out_offset=bass.IndirectOffsetOnAxis(ap=rk_idx[:, a:a + 1], axis=0),
                            in_=rk_val[:, a:a + 1], in_offset=None).then_inc(rank_out, 16)
                        pool.wait_ge(rank_out, 32 * t + (16 * a + 16))
                        pool.nop(nofuse=True)
                pool.wait_ge(rank_out, 32 * ETILES)
                pool.nop(nofuse=True)
            nc.gpsimd.memset(ends[0:1, 0, 0:1], 0.0).then_inc(edges_sorted, 1)
            pool.wait_ge(runs_made, 16 * CHUNKS)
            pool.wait_ge(tile_tables, 1)
            pool.nop(nofuse=True)
            for a in range(2):
                nc.gpsimd.indirect_dma_start(
                    out=rows_i[:, a, :], out_offset=None,
                    in_=runs.rearrange("c a (t e) -> (c a t) e", e=P),
                    in_offset=bass.IndirectOffsetOnAxis(ap=run_idx[0:TPAD, a:a + 1], axis=0)
                ).then_inc(rows_in, 16)

            pool.wait_ge(src_ready, 1)

            def gathers(phase, l):
                pool.wait_ge(table_stored, 16 * CHUNKS * (l + 1))
                if phase % 2 == 0:
                    pool.wait_ge(ohT_ready, 1)
                if phase == 2:
                    pool.wait_ge(h_ready, CHUNKS)
                with pool.Fori(0, TURNS) as i:
                    for u in range(UN):
                        pool.wait_ge(g_free[u], i + (1 + TURNS * phase))
                        pool.nop(nofuse=True)
                        nc.gpsimd.tensor_copy(idx_now[:, u:u + 1], src_i[:, bass.ds(i * UN + u, 1)]
                                              ).then_inc(idx_set, 1)
                        pool.wait_ge(idx_set, i * UN + (u + 1 + TILES * phase))
                        pool.nop(nofuse=True)
                        nc.gpsimd.indirect_dma_start(
                            out=gat[:, u, :], out_offset=None, in_=tables[l],
                            in_offset=bass.IndirectOffsetOnAxis(ap=idx_now[:, u:u + 1], axis=0)
                        ).then_inc(gathered[u], 16)

            for l in range(2):
                gathers(2 * l, l)
                gathers(2 * l + 1, l)
                if l == 1:
                    pool.wait_ge(norm_in, 64)
                    pool.wait_ge(h_ready, CHUNKS)
                    for c in range(CHUNKS):
                        nc.gpsimd.tensor_tensor(x_sb[:, c, :], x_sb[:, c, :], ln_b[:, :], ALU.add
                                                ).then_inc(xb_ready, 1)
                for c in range(CHUNKS):
                    pool.wait_ge(normed, CHUNKS * l + c + 1)
                    if c >= EB:
                        pool.wait_ge(elu_used, CHUNKS * l + c - EB + 1)
                    pm = posm[:, c % EB, :]
                    nc.gpsimd.tensor_scalar(pm, v_sb[:, c, :], 0.0, -1.0, ALU.max, ALU.add).then_inc(pos_ready, 1)
                    if l == 0:
                        pool.wait_ge(pos_ready, 2 * c + 1)
                        nc.gpsimd.tensor_tensor(pm, pm, x_sb[:, c, :], ALU.add).then_inc(pos_ready, 1)

        @block.scalar
        def _(act):
            w_rows = lambda w: w.rearrange("(k p) n -> p k n", p=P)
            act.dma_start(x_sb[:, 0, :], x[0:P, :]).then_inc(x_in[0], 16)
            for a in range(2):
                at = slice(a * HALF, (a + 1) * HALF)
                act.dma_start(w_s[:, :, at], w_rows(w1s)[:, :, at]).then_inc(ws_in[a], 16)
            act.dma_start(x_sb[:, 1, :], x[P:2 * P, :]).then_inc(x_in[1], 16)
            act.dma_start(w_d[:, :, :], w_rows(w1d)).then_inc(wd_in, 16)
            act.wait_ge(pads_set, 4)
            for c in range(2, CHUNKS):
                n = P if c < CHUNKS - 1 else LAST
                act.dma_start(x_sb[0:n, c, :], x[c * P:c * P + n, :]).then_inc(x_in[c], 16)
            act.dma_start(bias_s[:, :], b1s.partition_broadcast(P)).then_inc(bias_in, 16)
            act.dma_start(bias_d[:, :], b1d.partition_broadcast(P)).then_inc(bias_in, 16)
            act.dma_start(attn[:, :], attn1.rearrange("h d -> (h d)").partition_broadcast(P)).then_inc(attn_in, 16)

            for l in range(2):
                for c in range(-2, CHUNKS):
                    if c >= 0:
                        for k in range(2):
                            act.wait_ge(row_ready[1], 2 * (CHUNKS * l + c) + k + 1)
                            nc.scalar.copy(fd3[:, c, k, :], stage_f[:, 1, :]).then_inc(fd_part, 1)
                    n = c + 2
                    if n < CHUNKS:
                        for half in range(2):
                            act.wait_ge(turned[half], CHUNKS * l + n + 1)
                            nc.scalar.copy(actT[:, 3 * half:3 * half + 3, n * P:(n + 1) * P],
                                           ps[:, TURN_PS[half]:TURN_PS[half] + 3 * P]
                                           .rearrange("p (k n) -> p k n", k=3)).then_inc(turn_copied[half], 1)

                if l == 0:
                    with act.Fori(0, TURNS) as i:
                        for u in range(UN):
                            act.wait_ge(f_free[u % FB], i * (UN // FB) + (u // FB + 2))
                            for h in range(DH, HEADS):
                                pr = prods[:, u % 2, h * HD:(h + 1) * HD]
                                last = nc.scalar.activation(
                                    pr, pr, ACT.Copy,
                                    accum_out=relu_sum[:, bass.ds(i * UN + u, 1), h:h + 1].rearrange("p a o -> p (a o)"))
                            last.then_inc(heads_act, 1)
                act.wait_ge(logits_turned, l + 1)
                nc.scalar.mul(lt, ps[:, 0:DIM].rearrange("p (g e) -> p g e", g=GROUPS), 1.0 - SLOPE
                              ).then_inc(lt_ready, 1)
                act.wait_ge(shifted, l + 1)
                nc.scalar.activation(mx2, lt, ACT.Exp).then_inc(exped, 1)
                act.wait_ge(ex_turned, l + 1)
                nc.scalar.copy(ex[:, :, :].rearrange("p t h -> p (t h)"), ps[:, 0:DIM]).then_inc(ex_ready, 1)
                for c in range(CHUNKS):
                    act.wait_ge(normed, CHUNKS * l + c + 1)
                    if c >= EB:
                        act.wait_ge(elu_used, CHUNKS * l + c - EB + 1)
                    nc.scalar.activation(ev[:, c % EB, :], v_sb[:, c, :], ACT.Exp).then_inc(v_exp, 1)
                act.wait_ge(var_ready, l + 1)
                nc.scalar.sqrt(root[:, :], var_e[:, :]).then_inc(root_ready, 1)
            act.wait_ge(var_ready, 3)
            nc.scalar.sqrt(root[:, :], var_e[:, :]).then_inc(root_ready, 1)

        @block.tensor
        def _(pe):
            for s in agg_free:
                pe.sem_inc(s, 1)
            pe.wait_ge(ident_set, 1)

            def turn_input(l, c):
                if l == 0:
                    pe.wait_ge(x_in[c], 16)
                else:
                    pe.wait_ge(h_ready, c + 1)
                for half in range(2):
                    if c > 0 or l > 0:
                        pe.wait_ge(turn_copied[half], CHUNKS * l + c)
                    for k in range(3):
                        at = TURN_PS[half] + k * P
                        mm = pe.transpose(ps[:, at:at + P],
                                          (x_sb, v_sb)[l][:, c, (3 * half + k) * P:(3 * half + k + 1) * P],
                                          ident[:, :])
                    mm.then_inc(turned[half], 1)

            def project(l, g):
                c, w = g // 2, (w_s, w_d)[g % 2]
                b = g % 2
                if g == 1:
                    pe.wait_ge(wd_in, 16 * (l + 1))
                pe.wait_ge(turn_copied[0], CHUNKS * l + c + 1)
                pe.wait_ge(turn_copied[1], CHUNKS * l + c + 1)
                if l > 0 or g >= 2:
                    pe.wait_ge(proj_free[b], CHUNKS * l + c)
                for half in range(2):
                    if g == 0:
                        pe.wait_ge(ws_in[half], 16 * (l + 1))
                    for k in range(KC):
                        mm = pe.matmul(ps[:, b * 1024 + half * 512:b * 1024 + half * 512 + HALF],
                                       actT[:, k, c * P:(c + 1) * P], w[:, k, half * HALF:(half + 1) * HALF],
                                       start=(k == 0), stop=(k == KC - 1))
                mm.then_inc(proj_ready[b], 1)

            def prepare():
                pe.wait_ge(rows_conv, 2)
                for a, at in ((0, SRC_PS), (1, DST_PS)):
                    pe.transpose(ps[:, at:at + TPAD], rows_f[:, a, :], ident[0:TPAD, 0:TPAD])
                for a, e in ((0, 0), (1, P - 1)):
                    mm = pe.matmul(ps[0:1, ENDS_PS + a * TPAD:ENDS_PS + (a + 1) * TPAD], rows_f[:, 1, e:e + 1],
                                   ident[0:TPAD, 0:TPAD], start=True, stop=True)
                mm.then_inc(rows_turned, 1)
                spread_dst(0)

            def spread_dst(a):
                if a == 1:
                    pe.wait_ge(spread_copied, 1)
                for g in range(3):
                    lhs = spread[:, (3 * a + g) * GT:(3 * a + g + 1) * GT, :].rearrange("p t h -> p (t h)")
                    mm = pe.matmul(ps[:, SPREAD_PS[a] + g * P:SPREAD_PS[a] + (g + 1) * P], lhs, rows_f[:, 1, :],
                                   start=True, stop=True)
                mm.then_inc(dst_spread, 1)

            def feature_sums(l):
                pe.wait_ge(fd_ready, 2 * CHUNKS * (l + 1))
                pe.wait_ge(ohT_ready, 1)
                pe.wait_ge(tile_tables, 2)
                pe.wait_ge(proj_free[0], CHUNKS * (l + 1))
                pe.wait_ge(proj_free[1], CHUNKS * (l + 1))
                with pe.Fori(0, TURNS) as i:
                    for u in range(UN):
                        b = u % FB
                        c = pe.value_load(ct_i[0:1, bass.ds(i * UN + u, 1)], min_val=0, max_val=CHUNKS - 1)
                        oh = ohT[:, bass.ds(i * UN + u, 1), :].rearrange("p a e -> p (a e)")
                        pe.wait_ge(f_free[b], i * (UN // FB) + (u // FB + 1 + UN // FB * TURNS * l))
                        mid = b * 1024 + 512
                        for lo, hi in ((0, SPLIT[l]), (SPLIT[l], ROW)):
                            at = mid - SPLIT[l] + lo
                            for k in range(3):
                                mm = pe.matmul(ps[:, at:at + hi - lo], oh,
                                               fd3[:, bass.ds(c, 1), k, lo:hi].rearrange("p a n -> p (a n)"),
                                               start=(k == 0), stop=(lo > 0 and k == 2))
                            if lo == 0:
                                pe.wait_ge(gathered[u], i * 16 + (16 + 16 * TURNS * 2 * l))
                                pe.matmul(ps[:, at:at + hi], ident[:, :], gat[:, u, 0:hi], start=False, stop=True)
                        mm.then_inc(f_ready[b], 1)

            def softmax_turns(l):
                pe.wait_ge(logits_ready, l + 1)
                for g in range(GROUPS):
                    mm = pe.transpose(ps[:, g * P:(g + 1) * P],
                                      logits[:, g * GT:(g + 1) * GT, :].rearrange("p t h -> p (t h)"), ident[:, :])
                mm.then_inc(logits_turned, 1)
                pe.wait_ge(tile_max, l + 1)
                for a, e in ((0, P - 1), (1, 0)):
                    for g in range(GROUPS):
                        at = 1024 * (a + 1) + g * P
                        mm = pe.matmul(ps[0:1, at:at + P], mx2[:, g, e:e + 1], ident[:, :], start=True, stop=True)
                mm.then_inc(ends_turned, 1)
                pe.wait_ge(chain_ready, 2 * (l + 1))
                for a in range(2):
                    for g in range(GROUPS):
                        at = 3072 + a * GROUPS + g
                        row = brow[0:1, a, g * P:(g + 1) * P]
                        mm = pe.matmul(ps[:, at:at + 1], row, ones[0:1, 0:1], start=True, stop=True)
                mm.then_inc(chain_spread, 1)
                pe.wait_ge(exped, l + 1)
                for g in range(GROUPS):
                    mm = pe.transpose(ps[:, g * P:(g + 1) * P], mx2[:, g, :], ident[:, :])
                mm.then_inc(ex_turned, 1)

            def aggregate(l):
                pe.wait_ge(ex_ready, l + 1)
                for bank in range(8):
                    pe.matmul(ps[:, bank * 512:(bank + 1) * 512], zero_w[:, :], zero_m[:, :],
                              start=True, stop=False, skip_group_check=True)
                with pe.Fori(0, TURNS) as i:
                    for u in range(UN):
                        b = u % 2
                        c = pe.value_load(ct_i[0:1, bass.ds(i * UN + u, 1)], min_val=0, max_val=CHUNKS - 1)
                        pe.wait_ge(agg_in[b], i * (UN // 2) + (u // 2 + 1 + UN // 2 * TURNS * l))
                        if l == 1:
                            pe.wait_ge(gathered[u], i * 16 + (16 + 16 * TURNS * 3))
                        for q in range(DIM // QW):
                            rhs = prods[:, b, q * QW:(q + 1) * QW] if l == 0 else gat[:, u, q * QW:(q + 1) * QW]
                            mm = pe.matmul(ps[:, bass.ds(c * DIM + q * QW, QW)], onehot[:, b, :], rhs,
                                           start=False, stop=False, skip_group_check=True)
                        mm.then_inc(g_free[u], 1)
                        den = ex[:, bass.ds(i * UN + u, 1), :].rearrange("p a h -> p (a h)") if l == 0 else ones[:, 0:HEADS]
                        pe.matmul(ps[:, bass.ds(c * HEADS + DEN, HEADS)], onehot[:, b, :], den,
                                  start=False, stop=False, skip_group_check=True).then_inc(agg_free[b], 1)
                for bank in range(8):
                    mm = pe.matmul(ps[:, bank * 512:(bank + 1) * 512], zero_w[:, :], zero_m[:, :],
                                   start=False, stop=True, skip_group_check=True)
                mm.then_inc(agg_done, 1)

            pe.wait_ge(stats_ready, 5)
            pe.matmul(ps[:, CNT_PS:CNT_PS + 5], ones[0:125, :], stat[0:125, :], start=True, stop=True
                      ).then_inc(counts_ready, 1)
            for l in range(2):
                turn_input(l, 0)
                for g in range(2 * CHUNKS):
                    project(l, g)
                    if g % 2 == 0 and g < 2 * CHUNKS - 2:
                        turn_input(l, g // 2 + 1)
                    if l == 0 and g == 0:
                        prepare()
                    if l == 0 and g == 1:
                        spread_dst(1)
                feature_sums(l)
                softmax_turns(l)
                aggregate(l)

        @block.vector
        def _(dve):
            steps = [0]

            def link(ins):
                dve.wait_ge(dve_step, mark(ins))

            def mark(ins):
                steps[0] += 1
                ins.then_inc(dve_step, 1)
                return steps[0]

            v = nc.vector
            for s in (*g_free, *f_free):
                dve.sem_inc(s, 1)
            dve.wait_ge(consts_set, 9)
            v.tensor_scalar(ident[:, :], iota_f[:, :], iota_p[:, 0:1], None, ALU.is_equal).then_inc(ident_set, 1)
            dve.wait_ge(ident_set, 1)
            link(v.memset(off[:, 0:1], 0.0))
            link(v.memset(off[:, 5:6], float(EDGES)))
            link(v.memset(run_step[:, 0:1], 0.0))
            link(v.memset(tile0[:, 0:1], 0.0))

            dve.wait_ge(keys_in, 32)
            link(v.tensor_copy(keys[0:125, :], keys_i[0:125, :]))
            v.scalar_tensor_tensor(out=junk[0:125, 0, :], in0=keys[0:125, 0:80], scalar=0.0, in1=keys[0:125, 1:81],
                                   op0=ALU.add, op1=ALU.is_gt, accum_out=stat[0:125, 0:1]).then_inc(stats_ready, 1)
            for c in range(1, CHUNKS):
                v.tensor_scalar(junk[0:125, c, :], keys[0:125, 0:80], float(c * P), None, ALU.is_lt,
                                ALU.add, accum_out=stat[0:125, c:c + 1]).then_inc(stats_ready, 1)
            dve.wait_ge(counts_ready, 1)
            v.tensor_copy(flag_i[:, :], ps[:, CNT_PS:CNT_PS + 1]).then_inc(flag_ready, 1)

            link(v.tensor_copy(off[:, 1:5], ps[:, CNT_PS + 1:CNT_PS + 5]))
            v.tensor_copy(off_i[:, :], off[:, :]).then_inc(run_starts, 1)
            link(v.tensor_tensor(seg_n[:, :], off[:, 1:6], off[:, 0:5], ALU.subtract))
            for c in range(CHUNKS):
                n = mark(v.tensor_scalar(junk[:, 5 + c, :], iota_128k[:, :], seg_n[:, c:c + 1], None, ALU.is_lt,
                                         ALU.add, accum_out=seg_t[:, c:c + 1]))
            dve.wait_ge(dve_step, n)
            n = mark(v.tensor_scalar(run_step[:, 1:5], seg_t[:, 0:4], -1.0, 2.0 * TPAD, ALU.mult, ALU.add))
            link(v.tensor_tensor_scan(tile0[:, 1:6], ones[:, 0:5], seg_t[:, :], 0.0, ALU.mult, ALU.add))
            n = mark(v.scalar_tensor_tensor(out=tile_p[:, 0:5], in0=tile0[:, 0:5], scalar=iota_p[:, 0:1],
                                            in1=run_step[:, :], op0=ALU.is_le, op1=ALU.mult, accum_out=run_base[:, :]))
            link(v.tensor_scalar(tile_p[:, 5:10], tile0[:, 0:5], iota_p[:, 0:1], None, ALU.is_le, ALU.add,
                                 accum_out=chunk_p[:, :]))
            for a in range(2):
                n = mark(v.tensor_scalar(run_idx[:, a:a + 1], run_base[:, :], iota_p[:, 0:1], float(a * TPAD),
                                         ALU.add, ALU.add))
            dve.wait_ge(dve_step, n)
            v.tensor_scalar(chunk_p[:, :], chunk_p[:, :], -1.0, float(P), ALU.add, ALU.mult).then_inc(tile_tables, 1)
            link(v.tensor_scalar(ct[:, :], iota_t[0:1, :], tile0[0:1, 1:2], None, ALU.is_ge))
            for c in range(2, CHUNKS):
                link(v.scalar_tensor_tensor(out=ct[:, :], in0=iota_t[0:1, :], scalar=tile0[0:1, c:c + 1],
                                            in1=ct[:, :], op0=ALU.is_ge, op1=ALU.add))
            v.tensor_copy(ct_i[:, :], ct[:, :]).then_inc(tile_tables, 1)

            dve.wait_ge(flag_ready, 1)
            unsorted = dve.value_load(flag_i[0:1, 0:1], min_val=0, max_val=EDGES)
            with dve.If(unsorted > 0):
                dve.wait_ge(rank_cols, 32)
                dve.wait_ge(rank_iota, 2)
                v.tensor_copy(rk_kcol, rk_col_i[:, 1, :]).then_inc(rank_iota, 1)
                dve.wait_ge(rank_iota, 3)
                v.scalar_tensor_tensor(out=rk_kcol, in0=rk_kcol, scalar=SORT_SHIFT, in1=rk_eno,
                                       op0=ALU.mult, op1=ALU.add).then_inc(rank_iota, 1)
                for b in range(RBLOCKS):
                    dve.wait_ge(rank_blk, 16 * (b + 1))
                    dve.wait_ge(rank_iota, 4 + 3 * b)
                    v.tensor_copy(rk_key, rk_int).then_inc(rank_iota, 1)
                    dve.wait_ge(rank_iota, 5 + 3 * b)
                    v.scalar_tensor_tensor(out=rk_key, in0=rk_key, scalar=SORT_SHIFT, in1=rk_iota,
                                           op0=ALU.mult, op1=ALU.add).then_inc(rank_iota, 1)
                    dve.wait_ge(rank_iota, 6 + 3 * b)
                    with dve.Fori(0, ETILES) as t:
                        v.tensor_scalar(rk_out, rk_key, rk_kcol[:, bass.ds(t, 1)], None, ALU.is_lt, ALU.add,
                                        accum_out=rk_cnt[:, bass.ds(t + b * ETILES, 1)]).then_inc(rank_tile, 1)
                        dve.wait_ge(rank_tile, t + (1 + b * ETILES))
                    v.tensor_scalar(rk_kcol, rk_kcol, float(-RB), None, ALU.add).then_inc(rank_iota, 1)
                    dve.wait_ge(rank_iota, 7 + 3 * b)
                    v.tensor_copy(scrap[0:1, 0:1], rk_kcol[0:1, 0:1]).then_inc(rank_used, 1)
                dve.wait_ge(rank_used, RBLOCKS)
                v.tensor_reduce(rk_pos, rk_cnt.rearrange("p (b t) -> p t b", b=RBLOCKS), AX_X, ALU.add
                                ).then_inc(rank_iota, 1)
                dve.wait_ge(rank_iota, 5 + 3 * RBLOCKS)
                v.tensor_copy(rk_pos_i[:, 0, :], rk_pos).then_inc(rank_iota, 1)
                v.tensor_scalar(rk_pos_i[:, 1, :], rk_pos, float(STAGE), None, ALU.add).then_inc(ranked, 1)
            link(v.memset(cont[:, 0:1], 0.0))

            def evacuate(l, g):
                c, b = g // 2, g % 2
                bias = (bias_s, bias_d)[b]
                if g == 0:
                    dve.wait_ge(bias_in, 32 * (l + 1))
                    dve.wait_ge(attn_in, 16 * (l + 1))
                dve.wait_ge(proj_ready[b], CHUNKS * l + c + 1)
                if b == 0 and (c > 0 or l > 0):
                    dve.wait_ge(table_stored, 16 * (CHUNKS * l + c))
                if b == 1 and (c > 0 or l > 0):
                    dve.wait_ge(fd_ready, 2 * (CHUNKS * l + c))
                v.tensor_tensor(stage_f[:, b, 0:DIM].rearrange("p (a n) -> p a n", a=2),
                                ps[:, b * 1024:(b + 1) * 1024].rearrange("p (a n) -> p a n", a=2)[:, :, 0:HALF],
                                bias[:, :].rearrange("p (a n) -> p a n", a=2), ALU.add).then_inc(proj_free[b], 1)
                dve.wait_ge(proj_free[b], CHUNKS * l + c + 1)
                link(v.tensor_tensor(prod[:, :], stage_f[:, b, 0:DIM], attn[:, :], ALU.mult))
                last = v.tensor_reduce(stage_f[:, b, DIM:ROW], prod[:, :].rearrange("p (h d) -> p h d", h=HEADS),
                                       AX_X, ALU.add)
                last.then_inc(row_ready[b], 1)
                if b == 1:
                    for k in range(2):
                        dve.wait_ge(fd_part, 2 * (CHUNKS * l + c) + k + 1)
                        if k == 0:
                            v.tensor_tensor(stage_f[:, 1, :], stage_f[:, 1, :], fd3[:, c, 0, :], ALU.subtract
                                            ).then_inc(row_ready[1], 1)
                        else:
                            v.tensor_tensor(fd3[:, c, 2, :], stage_f[:, 1, :], fd3[:, c, 1, :], ALU.subtract
                                            ).then_inc(fd_ready, 2)

            def tile_rows():
                dve.wait_ge(rows_in, 32)
                dve.wait_ge(tile_tables, 2)
                v.tensor_copy(rows_f[:, 0, :], rows_i[:, 0, :]).then_inc(rows_conv, 1)
                v.tensor_scalar(rows_f[:, 1, :], rows_i[:, 1, :], chunk_p[0:TPAD, 0:1], None, ALU.subtract
                                ).then_inc(rows_conv, 1)
                dve.wait_ge(rows_conv, 2)
                v.tensor_copy(rel_b[:, :], rows_f[:, 1, :]).then_inc(rows_conv, 1)

            def tile_columns():
                n = TPAD
                dve.wait_ge(rows_turned, 1)
                v.tensor_copy(src_i[:, :], ps[:, SRC_PS:SRC_PS + n]).then_inc(src_ready, 1)
                link(v.tensor_copy(dst_rel[:, :], ps[:, DST_PS:DST_PS + n]))
                link(v.tensor_copy(ends[:, :, :], ps[0:1, ENDS_PS:ENDS_PS + 2 * n].rearrange("p (a t) -> p a t", a=2)))
                dve.wait_ge(dst_spread, 1)
                v.tensor_copy(dst_ht[:, 0:3, :], ps[:, SPREAD_PS[0]:SPREAD_PS[0] + HALF]
                              .rearrange("p (g e) -> p g e", g=3)).then_inc(spread_copied, 1)
                link(v.tensor_tensor(single[:, :], ends[:, 0, :], ends[:, 1, :], ALU.is_equal))
                link(v.tensor_tensor(cont[:, 1:n], ends[:, 0, 1:n], ends[:, 1, 0:n - 1], ALU.is_equal))
                link(v.tensor_tensor(tmp_row[:, 1:n], ct[0:1, 1:n], ct[0:1, 0:n - 1], ALU.is_equal))
                link(v.tensor_tensor(cont[:, 1:n], cont[:, 1:n], tmp_row[:, 1:n], ALU.mult))
                cp = chain_pen
                link(v.memset(cp[:, :, :], 0.0))
                link(v.tensor_tensor(cp[:, 0, 1:n], single[:, 0:n - 1], cont[:, 1:n], ALU.mult))
                link(v.tensor_copy(cp[:, 1, 1:n], cont[:, 1:n]))
                link(v.tensor_tensor(cp[:, 2, 0:n - 1], single[:, 1:n], cont[:, 1:n], ALU.mult))
                link(v.tensor_copy(cp[:, 3, 0:n - 1], cont[:, 1:n]))
                link(v.tensor_scalar(cp[:, :, :], cp[:, :, :], -NO, NO, ALU.mult, ALU.add))
                for a in range(2):
                    link(v.tensor_copy(chain_a[:, a, :, :], cp[:, 2 * a:2 * a + 1, :].to_broadcast([1, HEADS, n])))

            def scan_penalties():
                dve.wait_ge(dst_spread, 2)
                v.tensor_copy(dst_ht[:, 3:6, :], ps[:, SPREAD_PS[1]:SPREAD_PS[1] + HALF]
                              .rearrange("p (g e) -> p g e", g=3)).then_inc(spread_copied, 1)
                dve.wait_ge(spread_copied, 2)
                d = dst_ht
                ends_of = lambda e: d[:, :, e:e + 1].to_broadcast([P, GROUPS, P])
                v.memset(pen[:, 0, :, 0:1], 1.0)
                v.memset(pen[:, 1, :, P - 1:P], 1.0)
                v.tensor_tensor(pen[:, 0, :, 1:P], d[:, :, 1:P], d[:, :, 0:P - 1], ALU.not_equal)
                v.tensor_tensor(pen[:, 1, :, 0:P - 1], d[:, :, 1:P], d[:, :, 0:P - 1], ALU.not_equal)
                v.tensor_tensor(pen[:, 2, :, :], d[:, :, :], ends_of(0), ALU.not_equal)
                link(v.tensor_tensor(pen[:, 3, :, :], d[:, :, :], ends_of(P - 1), ALU.not_equal))
                flat = pen[:, :, :, :].rearrange("p a g e -> p (a g e)")
                link(v.tensor_scalar(flat, flat, NO, None, ALU.mult))

            def fd_onehots():
                dve.wait_ge(dstbc_in, 16)
                v.tensor_scalar(ohT[:, :, :].rearrange("p t e -> p (t e)"), dst_bc, iota_p[:, 0:1], None,
                                ALU.is_equal).then_inc(ohT_ready, 1)

            def edge_logits(l):
                def turn(i, first):
                    for u in range(UN):
                        b = u % FB
                        n = i * (UN // FB) + (u // FB + UN // FB * TURNS * l)
                        t = i * UN + u
                        dve.wait_ge(f_ready[b], n + 1)
                        dve.wait_ge(gathered[u], i * 16 + (16 + 16 * TURNS * 2 * l))
                        mid = b * 1024 + 512
                        at = mid - SPLIT[l]
                        rest = ps[:, mid:at + DIM]
                        v.tensor_tensor(rest, rest, gat[:, u, SPLIT[l]:DIM], ALU.add).then_inc(sum_ready, 1)
                        v.tensor_tensor(lin[:, bass.ds(t, 1), :].rearrange("p a h -> p (a h)"),
                                        ps[:, at + DIM:at + ROW], gat[:, u, DIM:ROW], ALU.add
                                        ).then_inc(g_free[u], 1)
                        if l == 0 and not (first and u == 0):
                            sum_heads(t - 1, (u - 1) % UN, i if u else i - 1)
                        weigh(i, t, u, first and u < 2)

                def weigh(i, t, u, early):
                    b = u % FB
                    dve.wait_ge(sum_ready, t + (1 + TILES * l))
                    if l == 0 and not early:
                        dve.wait_ge(heads_act, t - 1)
                        dve.wait_ge(heads_dve, t - 1)
                    if l == 1 and not early:
                        dve.wait_ge(f_free[(u - 2) % FB],
                                    i * (UN // FB) + (UN // FB * TURNS * l + (u - 2) // FB + 2))
                    acc = dict(accum_out=relu_sum[:, bass.ds(t, 1), 0:1].rearrange("p a o -> p (a o)")) if l else {}
                    at = b * 1024 + 512 - SPLIT[l]
                    v.scalar_tensor_tensor(out=prods[:, u % 2, :], in0=ps[:, at:at + DIM], scalar=0.0,
                                           in1=attn[:, :], op0=ALU.max, op1=ALU.mult, **acc).then_inc(f_free[b], 1)

                def sum_heads(t, u, i):
                    dve.wait_ge(f_free[u % FB], i * (UN // FB) + (u // FB + 2))
                    v.tensor_reduce(relu_sum[:, bass.ds(t, 1), 0:DH].rearrange("p a h -> p (a h)"),
                                    prods[:, u % 2, 0:DH * HD].rearrange("p (h d) -> p h d", h=DH), AX_X, ALU.add
                                    ).then_inc(heads_dve, 1)

                turn(0, True)
                with dve.Fori(1, TURNS) as i:
                    turn(i, False)
                if l == 0:
                    sum_heads(TILES - 1, UN - 1, TURNS - 1)

            def softmax(l):
                for u in range(UN):
                    dve.wait_ge(g_free[u], TURNS * (2 * l + 1) + 1)
                if l == 0:
                    dve.wait_ge(heads_dve, TILES)
                    dve.wait_ge(heads_act, TILES)
                    v.scalar_tensor_tensor(out=logits[:, :, :], in0=lin[:, :, :], scalar=SLOPE / (1.0 - SLOPE),
                                           in1=relu_sum[:, :, :], op0=ALU.mult, op1=ALU.add
                                           ).then_inc(logits_ready, 1)
                else:
                    for b in range(FB):
                        dve.wait_ge(f_free[b], 2 * TURNS * (UN // FB) + 1)
                    link(v.tensor_reduce(scrap[:, 0:TPAD], lin[:, :, :], AX_X, ALU.add))
                    v.scalar_tensor_tensor(
                        out=logits[:, :, 0], in0=scrap[:, 0:TPAD], scalar=SLOPE / (1.0 - SLOPE),
                        in1=relu_sum[:, :, 0], op0=ALU.mult, op1=ALU.add).then_inc(logits_ready, 1)
                flat = lambda a: a.rearrange("p g e -> p (g e)")
                dve.wait_ge(lt_ready, l + 1)
                link(v.tensor_tensor_scan(flat(mx), flat(pen[:, 0, :, :]), flat(lt), NO, ALU.add, ALU.max))
                v.tensor_tensor_scan(flat(mx2)[:, ::-1], flat(pen[:, 1, :, :])[:, ::-1], flat(mx)[:, ::-1],
                                     NO, ALU.add, ALU.max).then_inc(tile_max, 1)
                dve.wait_ge(ends_turned, l + 1)
                n = TPAD
                hm = lambda r, a: r[0:1, a, :].rearrange("p (h t) -> p h t", h=HEADS)
                for a in range(2):
                    link(v.tensor_copy(hm(mrow, a), ps[0:1, 1024 * (a + 1):1024 * (a + 1) + DIM]
                                       .rearrange("p (t h) -> p h t", h=HEADS)))
                link(v.memset(brow[0:1, :, :], NO))
                link(v.tensor_tensor(hm(brow, 0)[:, :, 1:n], hm(mrow, 0)[:, :, 0:n - 1],
                                     chain_pen[:, 1:2, 1:n].to_broadcast([1, HEADS, n - 1]), ALU.add))
                link(v.tensor_tensor(hm(brow, 1)[:, :, 0:n - 1], hm(mrow, 1)[:, :, 1:n],
                                     chain_pen[:, 3:4, 0:n - 1].to_broadcast([1, HEADS, n - 1]), ALU.add))
                ca = chain_a[:, :, :, :].rearrange("p a h t -> p a (h t)")
                link(v.tensor_tensor_scan(srow[0:1, 0, :], ca[:, 0, :], brow[0:1, 0, :], NO, ALU.add, ALU.max))
                link(v.tensor_tensor_scan(srow[0:1, 1, ::-1], ca[:, 1, ::-1], brow[0:1, 1, ::-1],
                                          NO, ALU.add, ALU.max))
                for a in range(2):
                    v.tensor_copy(brow[0:1, a, :].rearrange("p (t h) -> p h t", h=HEADS), hm(srow, a)
                                  ).then_inc(chain_ready, 1)
                dve.wait_ge(chain_spread, l + 1)
                link(v.tensor_copy(carry, ps[:, 3072:3072 + 2 * GROUPS]))
                for a, (i0, o) in enumerate(((mx2, mx), (mx, mx2))):
                    for g in range(GROUPS):
                        link(v.scalar_tensor_tensor(
                            out=o[:, g, :], in0=pen[:, 2 + a, g, :], scalar=carry[:, a * GROUPS + g:a * GROUPS + g + 1],
                            in1=i0[:, g, :], op0=ALU.add, op1=ALU.max))
                v.tensor_tensor(lt, lt, mx2, ALU.subtract).then_inc(shifted, 1)

            def aggregation_inputs(l):
                dve.wait_ge(ex_ready, l + 1)
                with dve.Fori(0, TURNS) as i:
                    for u in range(UN):
                        b = u % 2
                        t = i * UN + u
                        dve.wait_ge(agg_free[b], i * (UN // 2) + (u // 2 + 1 + UN // 2 * TURNS * l))
                        if l == 0:
                            v.tensor_scalar(onehot[:, b, :], iota_f[:, :], dst_rel[:, bass.ds(t, 1)], None,
                                            ALU.is_equal)
                            dve.wait_ge(gathered[u], i * 16 + (16 + 16 * TURNS))
                            v.tensor_tensor(prods[:, b, :].rearrange("p (h d) -> p h d", h=HEADS),
                                            gat[:, u, 0:DIM].rearrange("p (h d) -> p h d", h=HEADS),
                                            ex[:, bass.ds(t, 1), :].rearrange("p a h -> p h a")
                                            .to_broadcast([P, HEADS, HD]), ALU.mult).then_inc(agg_in[b], 1)
                        else:
                            v.tensor_scalar(onehot[:, b, :], iota_f[:, :], dst_rel[:, bass.ds(t, 1)],
                                            ex[:, bass.ds(t, 1), 0:1].rearrange("p a o -> p (a o)"),
                                            ALU.is_equal, ALU.mult).then_inc(agg_in[b], 1)

            def moments(c):
                for a in range(2):
                    n = mark(v.bn_stats(bn6[:, c, a, :], v_sb[:, c, a * HALF:(a + 1) * HALF]))
                dve.wait_ge(dve_step, n)
                return mark(v.bn_aggr(mv[:, c, :], bn6[:, c, :, :].rearrange("p a s -> p (a s)")))

            def inverse_deviation(n):
                dve.wait_ge(root_ready, n)
                link(v.reciprocal(rstd[:, :], root[:, :]))
                link(v.tensor_tensor(nt1[:, :], rstd[:, :], rstd[:, :], ALU.mult))
                link(v.tensor_tensor(nt1[:, :], nt1[:, :], var_e[:, :], ALU.mult))
                link(v.tensor_scalar(nt1[:, :], nt1[:, :], -0.5, 1.5, ALU.mult, ALU.add))
                link(v.tensor_tensor(rstd[:, :], rstd[:, :], nt1[:, :], ALU.mult))

            def nodes(l):
                dve.wait_ge(agg_done, l + 1)
                link(v.tensor_scalar(rden[:, :], ps[:, DEN:DEN + CHUNKS * HEADS], TINY, None, ALU.max))
                link(v.reciprocal(rden[:, :], rden[:, :]))
                for c in range(CHUNKS):
                    v.tensor_tensor(v_sb[:, c, :].rearrange("p (h d) -> p h d", h=HEADS),
                                    ps[:, c * DIM:(c + 1) * DIM].rearrange("p (h d) -> p h d", h=HEADS),
                                    rden[:, c * HEADS:(c + 1) * HEADS].rearrange("p (h o) -> p h o", o=1)
                                    .to_broadcast([P, HEADS, HD]), ALU.mult).then_inc(normed, 1)
                for c in range(CHUNKS):
                    dve.wait_ge(v_exp, CHUNKS * l + c + 1)
                    dve.wait_ge(pos_ready, 2 * (c + 1) if l == 0 else 2 * CHUNKS + c + 1)
                    v.scalar_tensor_tensor(out=v_sb[:, c, :], in0=ev[:, c % EB, :], scalar=1.0,
                                           in1=posm[:, c % EB, :], op0=ALU.min, op1=ALU.add).then_inc(elu_used, 1)
                    if c > 0:
                        dve.wait_ge(elu_used, CHUNKS * l + c)
                        moments(c - 1)
                dve.wait_ge(elu_used, CHUNKS * (l + 1))
                n = moments(CHUNKS - 1)
                dve.wait_ge(dve_step, n)
                v.tensor_scalar(var_e[:, :], mv[:, :, 1], EPS, None, ALU.add).then_inc(var_ready, 1)
                dve.wait_ge(norm_in, 32 * (l + 1))
                for c in range(CHUNKS):
                    scaled = mark(v.scalar_tensor_tensor(out=v_sb[:, c, :], in0=v_sb[:, c, :], scalar=mv[:, c, 0:1],
                                                         in1=ln_w[:, :], op0=ALU.subtract, op1=ALU.mult))
                inverse_deviation(l + 1)
                dve.wait_ge(dve_step, scaled)
                if l == 1:
                    dve.wait_ge(xb_ready, CHUNKS)
                for c in range(CHUNKS):
                    last = v.scalar_tensor_tensor(out=v_sb[:, c, :], in0=v_sb[:, c, :], scalar=rstd[:, c:c + 1],
                                                  in1=ln_b[:, :] if l == 0 else x_sb[:, c, :],
                                                  op0=ALU.mult, op1=ALU.add)
                    if l == 0:
                        last.then_inc(h_ready, 1)
                    else:
                        done = mark(last)
                        if c > 0:
                            dve.wait_ge(dve_step, before)
                            moments(c - 1)
                        before = done
                if l == 1:
                    dve.wait_ge(dve_step, before)
                    n = moments(CHUNKS - 1)
                    dve.wait_ge(dve_step, n)
                    v.tensor_scalar(var_e[:, :], mv[:, :, 1], EPS, None, ALU.add).then_inc(var_ready, 1)
                    inverse_deviation(3)
                    for c in range(CHUNKS):
                        v.tensor_scalar(v_sb[:, c, :], v_sb[:, c, :], mv[:, c, 0:1], rstd[:, c:c + 1],
                                        ALU.subtract, ALU.mult).then_inc(out_ready, 1)

            link(v.tensor_copy(spread, ident[0:TPAD, 0:TPAD].rearrange("p (t o) -> p t o", o=1)
                               .to_broadcast([TPAD, TPAD, HEADS])))
            tile_rows()
            for l in range(2):
                for g in range(2 * CHUNKS):
                    evacuate(l, g)
                    if l == 0 and g == 0:
                        tile_columns()
                    if l == 0 and g == 1:
                        scan_penalties()
                    if l == 0 and g == 3:
                        fd_onehots()
                edge_logits(l)
                softmax(l)
                aggregation_inputs(l)
                nodes(l)


_INS = ['x', 'src', 'dst', 'L0_gnn_W1s', 'L0_gnn_b1s', 'L0_gnn_W1d', 'L0_gnn_b1d', 'L0_gnn_attn1',
        'L0_gnn_ln1_w', 'L0_gnn_ln1_b', 'L0_gnn_Wos', 'L0_gnn_bos', 'L0_gnn_Wod', 'L0_gnn_bod',
        'L0_gnn_attno', 'L0_gnn_lno_w', 'L0_gnn_lno_b']
_OUTS = [((NODES, DIM), 'float32')]


def kernel(**inputs):
    import numpy as _np
    import concourse.bacc as _bacc
    from concourse import mybir as _mybir
    from concourse.bass_utils import run_bass_kernel_spmd as _run

    nc = _bacc.Bacc("TRN2", target_bir_lowering=False, num_devices=1)
    arrays, args = {}, []
    for name in _INS:
        a = _np.ascontiguousarray(inputs[name])
        arrays[f"in_{name}_dram"] = a
        args.append(nc.dram_tensor(f"in_{name}_dram", a.shape, _mybir.dt.from_np(a.dtype), kind="ExternalInput").ap())
    for i, (shape, dtype) in enumerate(_OUTS):
        dt = _mybir.dt.from_np(_np.dtype(dtype))
        args.append(nc.dram_tensor(f"out_{i}_dram", shape, dt, kind="ExternalOutput").ap())
    gat_kernel(nc, *args)
    r = _run(nc, [arrays], core_ids=[0])
    got = tuple(r.results[0][f"out_{i}_dram"] for i in range(len(_OUTS)))
    return got[0]
```

```python
from contextlib import ExitStack

import concourse.bass as bass
from concourse import mybir

ALU = mybir.AluOpType
ACT = mybir.ActivationFunctionType
AX_X = mybir.AxisListType.X
F32 = mybir.dt.float32
BF16 = mybir.dt.bfloat16
I32 = mybir.dt.int32

P = 128
NODES, EDGES, DIM, HEADS = 625, 10000, 768, 8
HD = DIM // HEADS
HALF = DIM // 2
KC = DIM // P
CHUNKS = -(-NODES // P)
LAST = NODES - (CHUNKS - 1) * P
TILES = 84
GROUPS = 6
GT = 16
TPAD = GROUPS * GT
ROW = DIM + HEADS
UN = 12
TURNS = TILES // UN
GB = 6
AB = 3
FB = 4
SPLIT = (400, 360)
EB = 2
DH = 2
QW = 256
DEN = CHUNKS * DIM
SLOTS = TPAD * P
STAGE = EDGES + SLOTS
PAD_DST = 1000.0
NO = -1.0e30
EPS = 1e-5
SLOPE = 0.2
SORT_SHIFT = 16384.0
ETILES = -(-EDGES // P)
RB = 1264
RBLOCKS = ETILES * P // RB
TINY = 1e-30
ACT_LAST = (1, 3)
SRC, DST = 0, 1
ORDER = ([(SRC, c) for c in range(CHUNKS)] + [(DST, c) for c in range(CHUNKS)],
         [(SRC, 0), (DST, 0), (SRC, 1), (DST, 1)] + [(SRC, c) for c in range(2, CHUNKS)]
         + [(DST, c) for c in range(2, CHUNKS)])
WARM = (6, 7, 5, 10, 5, 4, 34)
RSQRT_BITS = 1597463007.0


def gat_kernel(nc, x, src, dst, w1s, b1s, w1d, b1d, attn1, ln1w, ln1b,
               wos, bos, wod, bod, attno, lnow, lnob, out):
    staged = nc.dram_tensor("staged_edges", [2, STAGE], I32, kind="Internal").ap()
    runs = nc.dram_tensor("chunk_runs", [CHUNKS, 2, SLOTS], I32, kind="Internal").ap()
    rel_rows = nc.dram_tensor("relative_dst", [TPAD, P], BF16, kind="Internal").ap()
    tables = [nc.dram_tensor(f"fs_table{l}", [NODES, ROW], F32, kind="Internal").ap() for l in range(2)]

    with ExitStack() as ctx:
        def sb(name, shape, dt):
            return ctx.enter_context(nc.sbuf_tensor(name, shape, dt))

        def sem(name):
            return ctx.enter_context(nc.semaphore(name))

        x_sb = sb("x_sb", [P, CHUNKS, DIM], F32)
        actT = sb("actT", [P, KC, CHUNKS * P], F32)
        w_s = sb("w_s", [P, KC, DIM], F32)
        w_d = sb("w_d", [P, KC, DIM], F32)
        attn = sb("attn", [P, DIM], F32)
        bias_s, bias_d, ln_w, ln_b = [sb(n, [P, DIM], F32) for n in ("bias_s", "bias_d", "ln_w", "ln_b")]
        fd3 = sb("fd3", [P, CHUNKS, 3, ROW], BF16)
        ohT = sb("ohT", [P, TILES, P], BF16)
        arena = sb("arena", [P, TILES * P], F32)
        ident = sb("ident", [P, P], F32)
        ones = sb("ones", [P, P], F32)
        minus_one = sb("minus_one", [P, 1], F32)
        iota_f = sb("iota_f", [P, P], F32)
        iota_t = sb("iota_t", [P, TPAD], F32)
        iota_128k = sb("iota_128k", [P, 80], F32)
        iota_p = sb("iota_p", [P, 1], F32)
        zero_w = sb("zero_w", [P, P], BF16)
        zero_m = sb("zero_m", [P, 512], BF16)
        pads = sb("pads", [P, 2, SLOTS // P], I32)
        keys_i = sb("keys_i", [P, 81], I32)
        keys = sb("keys", [P, 81], F32)
        scrap = sb("scrap", [P, 128], F32)
        stat = sb("stat", [P, 5], F32)
        flag_i = sb("flag_i", [P, 1], I32)
        off = sb("off", [P, 6], F32)
        seg_n = sb("seg_n", [P, 5], F32)
        seg_t = sb("seg_t", [P, 5], F32)
        run_step = sb("run_step", [P, 5], F32)
        tile_p = sb("tile_p", [P, 10], F32)
        run_base = sb("run_base", [P, 1], F32)
        chunk_p = sb("chunk_p", [P, 1], F32)
        run_idx = sb("run_idx", [P, 2], I32)
        tile0 = sb("tile0", [P, 6], F32)
        off_i = sb("off_i", [P, 6], I32)
        ct = sb("ct", [HEADS, TPAD], F32)
        ct_i = sb("ct_i", [1, TPAD], I32)
        rows_i = sb("rows_i", [TPAD, 2, P], I32)
        rows_f = sb("rows_f", [TPAD, 2, P], F32)
        rel_b = sb("rel_b", [TPAD, P], BF16)
        end_cols = sb("end_cols", [TPAD, 2, HEADS], F32)
        src_i = sb("src_i", [P, TPAD], I32)
        dst_rel = sb("dst_rel", [P, TPAD], F32)
        pen = sb("pen", [P, 4, GROUPS, P], BF16)
        ends = sb("ends", [HEADS, 2, TPAD], F32)
        single = sb("single", [HEADS, TPAD], F32)
        cont = sb("cont", [HEADS, TPAD], F32)
        tmp_row = sb("tmp_row", [HEADS, TPAD], F32)
        chain_pen = sb("chain_pen", [HEADS, 4, TPAD], F32)
        brow = sb("brow", [HEADS, 2, TPAD], F32)
        srow = sb("srow", [HEADS, 2, TPAD], F32)
        tile_of = sb("tile_of", [P, GT], F32)
        head_of = sb("head_of", [P, HEADS], F32)
        head_ofT = sb("head_ofT", [HEADS, GT, HEADS], F32)
        relu_sum = sb("relu_sum", [P, TPAD, HEADS], F32)
        lin = sb("lin", [P, TPAD, HEADS], F32)
        logits = sb("logits", [P, TPAD, HEADS], F32)
        ex = sb("ex", [P, TPAD, HEADS], F32)
        ex3 = sb("ex3", [P, TPAD, 3, HEADS], BF16)
        idx_now = sb("idx_now", [P, GB], I32)
        rden = sb("rden", [P, CHUNKS * HEADS], F32)
        bn6 = sb("bn6", [P, CHUNKS, 2, 6], F32)
        mv = sb("mv", [P, CHUNKS, 2], F32)
        var_e = sb("var_e", [P, CHUNKS], F32)
        newton = sb("newton", [P, CHUNKS], F32)
        shift_by = sb("shift_by", [P, CHUNKS], F32)
        rstd = sb("rstd", [P, CHUNKS], F32)

        ps = ctx.enter_context(nc.psum_tensor("ps", [P, 4096], F32))

        def part(at, *shape):
            n = 1
            for s in shape:
                n *= s
            v = arena[:, at:at + n]
            if len(shape) == 2:
                return v.rearrange("p (a b) -> p a b", a=shape[0])
            if len(shape) == 3:
                return v.rearrange("p (a b c) -> p a b c", a=shape[0], b=shape[1])
            return v

        dst_bc = arena[:, 0:TILES * P // 2].bitcast(BF16)
        at_prep = 6400
        spread = part(at_prep, TPAD, HEADS)[0:TPAD]
        junk = part(at_prep + DIM, 10, 80)
        dst_ht = part(TILES * P // 2, GROUPS, P)
        stage_f = part(at_prep + DIM + 800, 2, ROW)
        prod = part(at_prep + DIM + 800 + 2 * ROW, DIM)
        gat = part(0, GB, ROW)
        prods = part(GB * ROW, AB, DIM)
        at_oh = GB * ROW + AB * DIM
        onehot = part(at_oh, AB, P)
        onehot_b = arena[:, at_oh + AB * P:at_oh + AB * P * 3 // 2].bitcast(BF16).rearrange("p (b n) -> p b n", b=AB)
        at_sm = at_oh + AB * P * 3 // 2
        mx = part(at_sm, GROUPS, P)
        mx2 = part(at_sm + DIM, GROUPS, P)
        ex_rest = part(at_sm + DIM, TPAD, HEADS)
        by_tile = part(at_sm + 2 * DIM, 2 * GROUPS, GT)
        carry = part(at_sm + 2 * DIM + 2 * TPAD, 2 * GROUPS)
        v_sb = part(0, CHUNKS, DIM)
        ev = part(CHUNKS * DIM, EB, DIM)
        posm = part((CHUNKS + EB) * DIM, EB, DIM)
        rk_int = arena[:, 0:RB].bitcast(I32)
        rk_key = arena[:, RB:2 * RB]
        rk_iota = arena[:, 2 * RB:3 * RB]
        rk_out = arena[:, 3 * RB:4 * RB]
        rk_cnt = arena[:, 4 * RB:4 * RB + RBLOCKS * ETILES]
        at_rk = 4 * RB + RBLOCKS * ETILES
        rk_col_i = arena[:, at_rk:at_rk + 2 * ETILES].bitcast(I32).rearrange("p (a t) -> p a t", a=2)
        rk_eno = arena[:, at_rk + 2 * ETILES:at_rk + 3 * ETILES]
        rk_kcol = arena[:, at_rk + 3 * ETILES:at_rk + 4 * ETILES]
        rk_pos = arena[:, at_rk + 4 * ETILES:at_rk + 5 * ETILES]
        rk_pos_i = arena[:, at_rk + 5 * ETILES:at_rk + 7 * ETILES].bitcast(I32).rearrange("p (a t) -> p a t", a=2)
        rk_idx = arena[:, at_rk + 7 * ETILES:at_rk + 7 * ETILES + 2].bitcast(I32)
        rk_val = arena[:, at_rk + 7 * ETILES + 2:at_rk + 7 * ETILES + 4].bitcast(I32)
        assert at_rk + 7 * ETILES + 4 <= at_prep

        pads_set = sem("pads_set")
        consts_set = sem("consts_set")
        ident_set = sem("ident_set")
        staged_in = sem("staged_in")
        keys_in = sem("keys_in")
        stats_ready = sem("stats_ready")
        counts_ready = sem("counts_ready")
        flag_ready = sem("flag_ready")
        rank_cols = sem("rank_cols")
        rank_blk = sem("rank_blk")
        rank_used = sem("rank_used")
        rank_iota = sem("rank_iota")
        ranked = sem("ranked")
        rank_tile = sem("rank_tile")
        rank_copy = sem("rank_copy")
        rank_out = sem("rank_out")
        edges_sorted = sem("edges_sorted")
        run_starts = sem("run_starts")
        tile_tables = sem("tile_tables")
        runs_made = sem("runs_made")
        rel_stored = sem("rel_stored")
        rows_in = sem("rows_in")
        dstbc_in = sem("dstbc_in")
        rows_conv = sem("rows_conv")
        rows_turned = sem("rows_turned")
        src_ready = sem("src_ready")
        dst_spread = sem("dst_spread")
        spread_copied = sem("spread_copied")
        ohT_ready = sem("ohT_ready")
        x_in = [sem(f"x_in{c}") for c in range(CHUNKS)]
        ws_in = [sem(f"ws_in{a}") for a in range(2)]
        wd_in = sem("wd_in")
        bias_in = sem("bias_in")
        norm_in = sem("norm_in")
        attn_in = sem("attn_in")
        turned = [sem(f"turned{b}") for b in range(2)]
        turn_copied = [sem(f"turn_copied{b}") for b in range(2)]
        proj_ready = [sem(f"proj_ready{b}") for b in range(2)]
        proj_free = [sem(f"proj_free{b}") for b in range(2)]
        row_ready = [sem(f"row_ready{b}") for b in range(2)]
        table_stored = sem("table_stored")
        fd_ready = sem("fd_ready")
        fd_part = sem("fd_part")
        gathered = [sem(f"gathered{u}") for u in range(GB)]
        g_free = [sem(f"g_free{u}") for u in range(GB)]
        idx_set = sem("idx_set")
        f_ready = [sem(f"f_ready{b}") for b in range(FB)]
        f_free = [sem(f"f_free{b}") for b in range(FB)]
        sum_ready = sem("sum_ready")
        heads_dve = sem("heads_dve")
        heads_act = sem("heads_act")
        logits_ready = sem("logits_ready")
        logits_turned = sem("logits_turned")
        ends_turned = sem("ends_turned")
        chain_ready = sem("chain_ready")
        chain_spread = sem("chain_spread")
        shifted = sem("shifted")
        ends_split = sem("ends_split")
        exped = sem("exped")
        ex_turned = sem("ex_turned")
        ex_ready = sem("ex_ready")
        ex_split = sem("ex_split")
        agg_in = [sem(f"agg_in{b}") for b in range(AB)]
        agg_free = [sem(f"agg_free{b}") for b in range(AB)]
        agg_done = sem("agg_done")
        normed = [sem(f"normed{c}") for c in range(CHUNKS)]
        v_exp = sem("v_exp")
        pos_ready = sem("pos_ready")
        elu_used = sem("elu_used")
        xb_ready = sem("xb_ready")
        relu_done = sem("relu_done")
        last_scale = sem("last_scale")
        relu_ready = sem("relu_ready")
        h_ready = sem("h_ready")
        out_ready = [sem(f"out_ready{c}") for c in range(CHUNKS)]
        out_stored = sem("out_stored")
        dve_step = sem("dve_step")

        TURN_PS = [(2048, 2560), (3072, 3584)]
        SPREAD_PS = [3584, 3072]
        SRC_PS, DST_PS, ENDS_PS, CNT_PS = 3072, 3072 + TPAD, 3072 + 2 * TPAD, 3984
        CHAIN_PS, CARRY_PS = 1024, 1536
        HG = GROUPS // 2
        HALVES = ((0, HG * GT // UN), (HG * GT // UN, TURNS))
        assert HG * GT % UN == 0

        def nth(i, u, n, more):
            return i * (UN // n) + (u // n + more)

        def landed(i, u, phase):
            return i * (16 * (UN // GB)) + 16 * (u // GB + 1 + TILES // GB * phase)

        block = ctx.enter_context(nc.Block())

        @block.sync
        def _(sp):
            sp.wait_ge(pads_set, 3)
            sp.dma_start(keys_i[0:125, 0:80], dst.rearrange("(p n) -> p n", p=125)).then_inc(keys_in, 16)
            with nc.allow_non_contiguous_dma("the first key of the next partition"):
                sp.dma_start(keys_i[0:124, 80:81], dst[80:EDGES].rearrange("(p n) -> p n", p=124)[:, 0:1]
                             ).then_inc(keys_in, 16)
            for a, v in enumerate((src, dst)):
                sp.dma_start(staged[a, 0:EDGES].rearrange("(b n) -> b n", b=16),
                             v.rearrange("(b n) -> b n", b=16)).then_inc(staged_in, 16)
                sp.dma_start(staged[a, EDGES:STAGE].rearrange("(p n) -> p n", p=P),
                             pads[:, a, :]).then_inc(staged_in, 16)
            sp.wait_ge(staged_in, 64)
            sp.wait_ge(edges_sorted, 1)
            sp.wait_ge(run_starts, 1)
            for c in range(CHUNKS):
                frm = sp.value_load(off_i[0:1, c:c + 1], min_val=0, max_val=EDGES) if c else 0
                sp.dma_start(runs[c, :, :].rearrange("a (b n) -> a b n", b=16),
                             staged[:, bass.ds(frm, SLOTS)].rearrange("a (b n) -> a b n", b=16)
                             ).then_inc(runs_made, 16)
            for l in range(2):
                for c in range(CHUNKS):
                    n = P if c < CHUNKS - 1 else LAST
                    sp.wait_ge(row_ready[0], 5 * l + c + 1)
                    sp.dma_start(tables[l][c * P:c * P + n, :], stage_f[0:n, 0, :]).then_inc(table_stored, 16)
                    if l == 0 and c == 1:
                        sp.wait_ge(rows_conv, 5)
                        sp.dma_start(rel_rows[:, :], rel_b[:, :]).then_inc(rel_stored, 16)
                if l == 0:
                    sp.wait_ge(rel_stored, 16)
                    sp.dma_start(dst_bc, rel_rows[0:TILES, :].rearrange("t e -> (t e)").partition_broadcast(P)
                                 ).then_inc(dstbc_in, 16)
                    sp.wait_ge(fd_ready, CHUNKS)
                    for k in range(KC):
                        sp.wait_ge(heads_act, 6 * (k + 1))
                        sp.dma_start(w_s[:, k, :], wos[k * P:(k + 1) * P, :]).then_inc(ws_in[0], 16)
                        sp.dma_start(w_d[:, k, :], wod[k * P:(k + 1) * P, :]).then_inc(wd_in, 16)
                    sp.dma_start(ln_w[:, :], ln1w.partition_broadcast(P)).then_inc(norm_in, 16)
                    sp.dma_start(ln_b[:, :], ln1b.partition_broadcast(P)).then_inc(norm_in, 16)
                    sp.wait_ge(logits_ready, 1)
                    sp.dma_start(attn[:, :], attno.rearrange("h d -> (h d)").partition_broadcast(P)
                                 ).then_inc(attn_in, 16)
                    sp.dma_start(bias_s[:, :], bos.partition_broadcast(P)).then_inc(bias_in, 16)
                    sp.dma_start(bias_d[:, :], bod.partition_broadcast(P)).then_inc(bias_in, 16)
                else:
                    sp.wait_ge(h_ready, CHUNKS)
                    sp.dma_start(ln_w[:, :], lnow.partition_broadcast(P)).then_inc(norm_in, 16)
                    sp.dma_start(ln_b[:, :], lnob.partition_broadcast(P)).then_inc(norm_in, 16)
            for c in range(CHUNKS):
                n = P if c < CHUNKS - 1 else LAST
                sp.wait_ge(out_ready[c], 1)
                sp.dma_start(out[c * P:c * P + n, :], v_sb[0:n, c, :]).then_inc(out_stored, 16)
            sp.wait_ge(out_stored, 16 * CHUNKS)

        @block.gpsimd
        def _(pool):
            nc.gpsimd.memset(pads[:, 0, :], 0).then_inc(pads_set, 1)
            nc.gpsimd.memset(pads[:, 1, :], int(PAD_DST)).then_inc(pads_set, 1)
            nc.gpsimd.memset(keys_i[:, 80:81], int(PAD_DST)).then_inc(pads_set, 1)
            nc.gpsimd.memset(x_sb[:, CHUNKS - 1, :], 0.0).then_inc(pads_set, 1)
            for dstt, pattern, mult in ((iota_f[:, :], [[1, P]], 0), (iota_p[:, :], [[1, 1]], 1),
                                        (iota_t[:, :], [[1, TPAD]], 0), (iota_128k[:, :], [[P, 80]], 0)):
                nc.gpsimd.iota(dstt, pattern, base=0, channel_multiplier=mult,
                               allow_small_or_imprecise_dtypes=True).then_inc(consts_set, 1)
            nc.gpsimd.memset(ones[:, :], 1.0).then_inc(consts_set, 1)
            nc.gpsimd.memset(minus_one[:, :], -1.0).then_inc(consts_set, 1)
            nc.gpsimd.memset(zero_w[:, :], 0.0).then_inc(consts_set, 1)
            nc.gpsimd.memset(zero_m[:, :], 0.0).then_inc(consts_set, 1)
            nc.gpsimd.memset(relu_sum[:, :, :], 0.0).then_inc(consts_set, 1)
            nc.gpsimd.memset(lin[:, :, :], 0.0).then_inc(consts_set, 1)

            pool.wait_ge(flag_ready, 1)
            unsorted = pool.value_load(flag_i[0:1, 0:1], min_val=0, max_val=EDGES)
            with pool.If(unsorted > 0):
                pool.wait_ge(staged_in, 64)
                with nc.allow_non_contiguous_dma("edges to columns"):
                    for a in range(2):
                        pool.dma_start(rk_col_i[:, a, :], staged[a, 0:ETILES * P]
                                       .rearrange("(t p) -> p t", p=P)).then_inc(rank_cols, 16)
                nc.gpsimd.iota(rk_iota, [[1, RB]], base=0, channel_multiplier=0,
                               allow_small_or_imprecise_dtypes=True).then_inc(rank_iota, 1)
                nc.gpsimd.iota(rk_eno, [[P, ETILES]], base=0, channel_multiplier=1,
                               allow_small_or_imprecise_dtypes=True).then_inc(rank_iota, 1)
                for b in range(RBLOCKS):
                    if b > 0:
                        pool.wait_ge(rank_used, b)
                    pool.dma_start(rk_int, staged[1, b * RB:(b + 1) * RB].partition_broadcast(P)
                                   ).then_inc(rank_blk, 16)
                pool.wait_ge(ranked, 1)
                with pool.Fori(0, ETILES) as t:
                    for a in range(2):
                        nc.gpsimd.tensor_copy(rk_idx[:, a:a + 1], rk_pos_i[:, a, bass.ds(t, 1)]
                                              ).then_inc(rank_copy, 1)
                        nc.gpsimd.tensor_copy(rk_val[:, a:a + 1], rk_col_i[:, a, bass.ds(t, 1)]
                                              ).then_inc(rank_copy, 1)
                        pool.wait_ge(rank_copy, 4 * t + 2 * a + 2)
                        pool.nop(nofuse=True)
                        nc.gpsimd.indirect_dma_start(
                            out=staged.rearrange("a (n o) -> (a n) o", o=1),
                            out_offset=bass.IndirectOffsetOnAxis(ap=rk_idx[:, a:a + 1], axis=0),
                            in_=rk_val[:, a:a + 1], in_offset=None).then_inc(rank_out, 16)
                        pool.wait_ge(rank_out, 32 * t + (16 * a + 16))
                        pool.nop(nofuse=True)
                pool.wait_ge(rank_out, 32 * ETILES)
                pool.nop(nofuse=True)
            nc.gpsimd.memset(ends[0:1, 0, 0:1], 0.0).then_inc(edges_sorted, 1)
            pool.wait_ge(runs_made, 16 * CHUNKS)
            pool.wait_ge(tile_tables, 1)
            pool.nop(nofuse=True)
            for a in range(2):
                nc.gpsimd.indirect_dma_start(
                    out=rows_i[:, a, :], out_offset=None,
                    in_=runs.rearrange("c a (t e) -> (c a t) e", e=P),
                    in_offset=bass.IndirectOffsetOnAxis(ap=run_idx[0:TPAD, a:a + 1], axis=0)
                ).then_inc(rows_in, 16)

            pool.wait_ge(src_ready, 1)

            def gathers(phase, l):
                pool.wait_ge(table_stored, 16 * CHUNKS * (l + 1))
                if phase % 2 == 0:
                    pool.wait_ge(ohT_ready, 1)
                if phase == 2:
                    pool.wait_ge(h_ready, CHUNKS)
                with pool.Fori(0, TURNS) as i:
                    for u in range(UN):
                        g = u % GB
                        pool.wait_ge(g_free[g], nth(i, u, GB, 1 + TILES // GB * phase))
                        pool.nop(nofuse=True)
                        nc.gpsimd.tensor_copy(idx_now[:, g:g + 1], src_i[:, bass.ds(i * UN + u, 1)]
                                              ).then_inc(idx_set, 1)
                        pool.wait_ge(idx_set, i * UN + (u + 1 + TILES * phase))
                        pool.nop(nofuse=True)
                        nc.gpsimd.indirect_dma_start(
                            out=gat[:, g, :], out_offset=None, in_=tables[l],
                            in_offset=bass.IndirectOffsetOnAxis(ap=idx_now[:, g:g + 1], axis=0)
                        ).then_inc(gathered[g], 16)

            for l in range(2):
                gathers(2 * l, l)
                gathers(2 * l + 1, l)
                if l == 1:
                    pool.wait_ge(norm_in, 64)
                    pool.wait_ge(h_ready, CHUNKS)
                    for c in range(CHUNKS):
                        nc.gpsimd.tensor_tensor(x_sb[:, c, :], x_sb[:, c, :], ln_b[:, :], ALU.add
                                                ).then_inc(xb_ready, 1)
                if l == 0:
                    for c in range(1, CHUNKS):
                        pm = posm[:, c % EB, :]
                        pool.wait_ge(relu_ready, c + 1)
                        nc.gpsimd.tensor_tensor(pm, pm, x_sb[:, c, :], ALU.add).then_inc(pos_ready, 1)

        @block.scalar
        def _(act):
            w_rows = lambda w: w.rearrange("(k p) n -> p k n", p=P)
            act.dma_start(x_sb[:, 0, :], x[0:P, :]).then_inc(x_in[0], 16)
            for a in range(2):
                at = slice(a * HALF, (a + 1) * HALF)
                act.dma_start(w_s[:, :, at], w_rows(w1s)[:, :, at]).then_inc(ws_in[a], 16)
                if a == 0:
                    act.dma_start(x_sb[:, 1, :], x[P:2 * P, :]).then_inc(x_in[1], 16)

            def copy_turned(l, n):
                for half in range(2):
                    act.wait_ge(turned[half], CHUNKS * l + n + 1)
                    nc.scalar.copy(actT[:, 3 * half:3 * half + 3, n * P:(n + 1) * P],
                                   ps[:, TURN_PS[l][half]:TURN_PS[l][half] + 3 * P]
                                   .rearrange("p (k n) -> p k n", k=3)).then_inc(turn_copied[half], 1)

            def split_fd(l, c):
                for k in range(2):
                    if k == 0:
                        at = ORDER[l].index((DST, c))
                        act.wait_ge(proj_free[at % 2], CHUNKS * l + at // 2 + 1)
                    else:
                        act.wait_ge(row_ready[1], CHUNKS * l + c + 1)
                    nc.scalar.copy(fd3[:, c, k, 0:DIM], stage_f[:, 1, 0:DIM]).then_inc(fd_part, 1)

            def elu_parts(l, c):
                pm = posm[:, c % EB, :]
                act.wait_ge(normed[c], l + 1)
                if c >= EB:
                    act.wait_ge(elu_used, CHUNKS * l + c - EB + 1)
                nc.scalar.activation(pm, v_sb[:, c, :], ACT.Relu).then_inc(relu_done, 1)
                act.wait_ge(relu_done, CHUNKS * l + c + 1)
                nc.scalar.activation(pm, pm, ACT.Identity, bias=minus_one[:, 0:1]).then_inc(relu_ready, 1)
                nc.scalar.activation(ev[:, c % EB, :], v_sb[:, c, :], ACT.Exp).then_inc(v_exp, 1)

            copy_turned(0, 0)
            act.dma_start(w_d[:, :, :], w_rows(w1d)).then_inc(wd_in, 16)
            act.wait_ge(pads_set, 4)
            for c in range(2, CHUNKS):
                n = P if c < CHUNKS - 1 else LAST
                act.dma_start(x_sb[0:n, c, :], x[c * P:c * P + n, :]).then_inc(x_in[c], 16)
            act.dma_start(bias_s[:, :], b1s.partition_broadcast(P)).then_inc(bias_in, 16)
            act.dma_start(bias_d[:, :], b1d.partition_broadcast(P)).then_inc(bias_in, 16)
            act.dma_start(attn[:, :], attn1.rearrange("h d -> (h d)").partition_broadcast(P)).then_inc(attn_in, 16)
            for c in range(1, CHUNKS):
                copy_turned(0, c)
            for c in range(CHUNKS):
                split_fd(0, c)
            for l in range(2):
                if l == 0:
                    with act.Fori(0, TURNS) as i:
                        for u in range(UN):
                            act.wait_ge(f_free[u % FB], nth(i, u, FB, 2))
                            for h in range(DH, HEADS):
                                pr = prods[:, u % 2, h * HD:(h + 1) * HD]
                                last = nc.scalar.activation(
                                    pr, pr, ACT.Copy,
                                    accum_out=relu_sum[:, bass.ds(i * UN + u, 1), h:h + 1].rearrange("p a o -> p (a o)"))
                            last.then_inc(heads_act, 1)
                for a in range(2):
                    at = slice(a * HG, (a + 1) * HG)
                    act.wait_ge(shifted, 2 * l + a + 1)
                    nc.scalar.activation(mx[:, at, :], mx[:, at, :], ACT.Exp, scale=1.0 - SLOPE).then_inc(exped, 1)
                    act.wait_ge(ex_turned, 2 * l + a + 1)
                    nc.scalar.copy(ex[:, a * HG * GT:(a + 1) * HG * GT, :].rearrange("p t h -> p (t h)"),
                                   ps[:, a * 512:a * 512 + HALF]).then_inc(ex_ready, 1)
                elu_parts(l, 0)
                elu_parts(l, 1)
                if l == 0:
                    copy_turned(1, 0)
                    elu_parts(0, 2)
                    elu_parts(0, 3)
                    elu_parts(0, 4)
                    copy_turned(1, 1)
                    split_fd(1, 0)
                    copy_turned(1, 2)
                    copy_turned(1, 3)
                    split_fd(1, 1)
                    copy_turned(1, 4)
                    for c in range(2, CHUNKS):
                        split_fd(1, c)
                else:
                    for c in range(2, CHUNKS):
                        elu_parts(1, c)
                    act.wait_ge(last_scale, 1)
                    for c in ACT_LAST:
                        nc.scalar.activation(v_sb[:, c, :], v_sb[:, c, :], ACT.Identity, bias=shift_by[:, c:c + 1],
                                             scale=rstd[:, c:c + 1]).then_inc(out_ready[c], 1)

        @block.tensor
        def _(pe):
            for s in agg_free:
                pe.sem_inc(s, 1)
            pe.wait_ge(ident_set, 1)

            def turn_input(l, c):
                if l == 0:
                    pe.wait_ge(x_in[c], 16)
                else:
                    pe.wait_ge(h_ready, c + 1)
                    pe.wait_ge(normed[CHUNKS - 1], 1)
                for half in range(2):
                    if c > 0 or l > 0:
                        pe.wait_ge(turn_copied[half], CHUNKS * l + c)
                    for k in range(3):
                        at = TURN_PS[l][half] + k * P
                        mm = pe.transpose(ps[:, at:at + P],
                                          (x_sb, v_sb)[l][:, c, (3 * half + k) * P:(3 * half + k + 1) * P],
                                          ident[:, :])
                    mm.then_inc(turned[half], 1)

            def project(l, k):
                (kind, c), b = ORDER[l][k], k % 2
                w = (w_s, w_d)[kind]
                if l == 1 and k == 1:
                    pe.wait_ge(normed[2], 1)
                if (kind, c) == (DST, 0):
                    pe.wait_ge(wd_in, 16 + 16 * KC * l)
                pe.wait_ge(turn_copied[0], CHUNKS * l + c + 1)
                pe.wait_ge(turn_copied[1], CHUNKS * l + c + 1)
                if l > 0 or k >= 2:
                    pe.wait_ge(proj_free[b], CHUNKS * l + k // 2)
                for half in range(2):
                    if k == 0 and (l == 0 or half == 0):
                        pe.wait_ge(ws_in[half], 16 + 16 * KC * l)
                    for kc in range(KC):
                        mm = pe.matmul(ps[:, b * 1024 + half * 512:b * 1024 + half * 512 + HALF],
                                       actT[:, kc, c * P:(c + 1) * P], w[:, kc, half * HALF:(half + 1) * HALF],
                                       start=(kc == 0), stop=(kc == KC - 1))
                mm.then_inc(proj_ready[b], 1)

            def prepare():
                pe.wait_ge(rows_conv, 4)
                for a, at in ((0, SRC_PS), (1, DST_PS)):
                    pe.transpose(ps[:, at:at + TPAD], rows_f[:, a, :], ident[0:TPAD, 0:TPAD])
                for a, e in ((0, 0), (1, P - 1)):
                    mm = pe.matmul(ps[0:HEADS, ENDS_PS + a * TPAD:ENDS_PS + (a + 1) * TPAD], end_cols[:, a, :],
                                   ident[0:TPAD, 0:TPAD], start=True, stop=True)
                mm.then_inc(rows_turned, 1)
                spread_dst(0)

            def spread_dst(a):
                if a == 1:
                    pe.wait_ge(spread_copied, 1)
                for g in range(3):
                    lhs = spread[:, (3 * a + g) * GT:(3 * a + g + 1) * GT, :].rearrange("p t h -> p (t h)")
                    mm = pe.matmul(ps[:, SPREAD_PS[a] + g * P:SPREAD_PS[a] + (g + 1) * P], lhs, rows_f[:, 1, :],
                                   start=True, stop=True)
                mm.then_inc(dst_spread, 1)

            def feature_sums(l):
                pe.wait_ge(ohT_ready, 1)
                pe.wait_ge(tile_tables, 2)
                pe.wait_ge(proj_free[0], CHUNKS * (l + 1))
                pe.wait_ge(proj_free[1], CHUNKS * (l + 1))

                def turn(i, first):
                    for u in range(UN):
                        b = u % FB
                        c = pe.value_load(ct_i[0:1, bass.ds(i * UN + u, 1)], min_val=0, max_val=CHUNKS - 1)
                        oh = ohT[:, bass.ds(i * UN + u, 1), :].rearrange("p a e -> p (a e)")
                        if first:
                            pe.wait_ge(fd_ready, c + (1 + CHUNKS * l))
                        pe.wait_ge(f_free[b], nth(i, u, FB, 1 + TILES // FB * l))
                        mid = b * 1024 + 512
                        for lo, hi in ((0, SPLIT[l]), (SPLIT[l], ROW)):
                            at = mid - SPLIT[l] + lo
                            for k in range(3):
                                mm = pe.matmul(ps[:, at:at + hi - lo], oh,
                                               fd3[:, bass.ds(c, 1), k, lo:hi].rearrange("p a n -> p (a n)"),
                                               start=(k == 0), stop=(lo > 0 and k == 2))
                            if lo == 0:
                                pe.wait_ge(gathered[u % GB], landed(i, u, 2 * l))
                                pe.matmul(ps[:, at:at + hi], ident[:, :], gat[:, u % GB, 0:hi],
                                          start=False, stop=True)
                        mm.then_inc(f_ready[b], 1)

                turn(0, True)
                pe.wait_ge(fd_ready, CHUNKS * (l + 1))
                with pe.Fori(1, TURNS) as i:
                    turn(i, False)

            def clear(banks):
                for bank in banks:
                    pe.matmul(ps[:, bank * 512:(bank + 1) * 512], zero_w[:, :], zero_m[:, :],
                              start=True, stop=False, skip_group_check=True)

            def keep_warm(bank, n):
                for _ in range(n):
                    pe.matmul(ps[:, bank * 512:(bank + 1) * 512], zero_w[:, :], zero_m[:, :],
                              start=True, stop=True, skip_group_check=True)

            def softmax_turns(l):
                for a in range(2):
                    pe.wait_ge(logits_ready, 2 * l + a + 1)
                    for g in range(HG):
                        t = (a * HG + g) * GT
                        mm = pe.transpose(ps[:, a * 512 + g * P:a * 512 + (g + 1) * P],
                                          logits[:, t:t + GT, :].rearrange("p t h -> p (t h)"), ident[:, :])
                    mm.then_inc(logits_turned, 1)
                    keep_warm(5, WARM[a])
                pe.wait_ge(ends_split, 2 * (l + 1))
                pe.matmul(ps[0:HEADS, CHAIN_PS:CHAIN_PS + 2 * TPAD], head_of[:, :],
                          by_tile.rearrange("p g t -> p (g t)"), start=True, stop=True).then_inc(ends_turned, 1)
                keep_warm(5, WARM[2])
                pe.wait_ge(chain_ready, 2 * (l + 1))
                pe.matmul(ps[:, CARRY_PS:CARRY_PS + 2 * TPAD], head_ofT[:, :, :].rearrange("p t h -> p (t h)"),
                          srow[:, :, :].rearrange("p a t -> p (a t)"), start=True, stop=True
                          ).then_inc(chain_spread, 1)
                keep_warm(5, WARM[3])
                clear(range(4, 8))
                for a in range(2):
                    pe.wait_ge(exped, 2 * l + a + 1)
                    for g in range(HG):
                        mm = pe.transpose(ps[:, a * 512 + g * P:a * 512 + (g + 1) * P], mx[:, a * HG + g, :],
                                          ident[:, :])
                    mm.then_inc(ex_turned, 1)
                    if a == 0:
                        keep_warm(5, WARM[4])

            def aggregate(l):
                clear(range(2, 4))
                pe.wait_ge(ex_ready, 2 * (l + 1))
                clear(range(2))
                keep_warm(5, WARM[5])

                def turn(i):
                    for u in range(UN):
                        b, g = u % AB, u % GB
                        c = pe.value_load(ct_i[0:1, bass.ds(i * UN + u, 1)], min_val=0, max_val=CHUNKS - 1)
                        pe.wait_ge(agg_in[b], nth(i, u, AB, 1 + TILES // AB * l))
                        for q in range(DIM // QW):
                            rhs = prods[:, b, q * QW:(q + 1) * QW] if l == 0 else gat[:, g, q * QW:(q + 1) * QW]
                            mm = pe.matmul(ps[:, bass.ds(c * DIM + q * QW, QW)], onehot[:, b, :], rhs,
                                           start=False, stop=False, skip_group_check=True)
                        mm.then_inc(g_free[g], 1)
                        pe.matmul(ps[:, bass.ds(c * (3 * HEADS) + DEN, 3 * HEADS)], onehot_b[:, b, :],
                                  ex3[:, bass.ds(i * UN + u, 1), :, :].rearrange("p t a h -> p (t a h)"),
                                  start=False, stop=False, skip_group_check=True).then_inc(agg_free[b], 1)

                for a, turns in enumerate(HALVES):
                    pe.wait_ge(ex_split, 2 * l + a + 1)
                    with pe.Fori(*turns) as i:
                        turn(i)
                for bank in range(8):
                    mm = pe.matmul(ps[:, bank * 512:bank * 512 + 1], zero_w[:, :], zero_m[:, 0:1],
                                   start=False, stop=True, skip_group_check=True)
                mm.then_inc(agg_done, 1)

            for l in range(2):
                if l == 1:
                    pe.wait_ge(normed[CHUNKS - 1], 1)
                    keep_warm(7, WARM[6])
                turned_up_to = -1
                for k in range(-2, 2 * CHUNKS):
                    if k >= 0:
                        project(l, k)
                    while k + 2 < 2 * CHUNKS and ORDER[l][k + 2][1] > turned_up_to:
                        if l == 0 and k == -1:
                            break
                        turned_up_to += 1
                        turn_input(l, turned_up_to)
                    if l == 0 and k == -2:
                        pe.wait_ge(stats_ready, 5)
                        pe.matmul(ps[:, CNT_PS:CNT_PS + 5], ones[0:125, :], stat[0:125, :], start=True, stop=True
                                  ).then_inc(counts_ready, 1)
                    if l == 0 and k == 2:
                        prepare()
                    if l == 0 and k == 3:
                        spread_dst(1)
                feature_sums(l)
                softmax_turns(l)
                aggregate(l)

        @block.vector
        def _(dve):
            steps = [0]

            def link(ins):
                dve.wait_ge(dve_step, mark(ins))

            def mark(ins):
                steps[0] += 1
                ins.then_inc(dve_step, 1)
                return steps[0]

            v = nc.vector
            for s in (*g_free, *f_free):
                dve.sem_inc(s, 1)
            dve.wait_ge(consts_set, 10)
            v.tensor_scalar(ident[:, :], iota_f[:, :], iota_p[:, 0:1], None, ALU.is_equal).then_inc(ident_set, 1)
            dve.wait_ge(ident_set, 1)
            link(v.memset(off[:, 0:1], 0.0))
            link(v.memset(off[:, 5:6], float(EDGES)))
            link(v.memset(run_step[:, 0:1], 0.0))
            link(v.memset(tile0[:, 0:1], 0.0))
            link(v.memset(brow[:, :, :], NO))
            link(v.tensor_reduce(tile_of[:, :], ident[:, :].rearrange("p (t h) -> p t h", h=HEADS), AX_X, ALU.add))
            link(v.tensor_reduce(head_of[:, :], ident[:, :].rearrange("p (t h) -> p h t", h=HEADS), AX_X, ALU.add))
            link(v.tensor_copy(head_ofT[:, :, :], ident[0:HEADS, 0:HEADS].rearrange("p (o h) -> p o h", o=1)
                               .to_broadcast([HEADS, GT, HEADS])))

            dve.wait_ge(keys_in, 32)
            link(v.tensor_copy(keys[0:125, :], keys_i[0:125, :]))
            v.scalar_tensor_tensor(out=junk[0:125, 0, :], in0=keys[0:125, 0:80], scalar=0.0, in1=keys[0:125, 1:81],
                                   op0=ALU.add, op1=ALU.is_gt, accum_out=stat[0:125, 0:1]).then_inc(stats_ready, 1)
            for c in range(1, CHUNKS):
                v.tensor_scalar(junk[0:125, c, :], keys[0:125, 0:80], float(c * P), None, ALU.is_lt,
                                ALU.add, accum_out=stat[0:125, c:c + 1]).then_inc(stats_ready, 1)
            dve.wait_ge(counts_ready, 1)
            v.tensor_copy(flag_i[:, :], ps[:, CNT_PS:CNT_PS + 1]).then_inc(flag_ready, 1)

            link(v.tensor_copy(off[:, 1:5], ps[:, CNT_PS + 1:CNT_PS + 5]))
            v.tensor_copy(off_i[:, :], off[:, :]).then_inc(run_starts, 1)
            link(v.tensor_tensor(seg_n[:, :], off[:, 1:6], off[:, 0:5], ALU.subtract))
            for c in range(CHUNKS):
                n = mark(v.tensor_scalar(junk[:, 5 + c, :], iota_128k[:, :], seg_n[:, c:c + 1], None, ALU.is_lt,
                                         ALU.add, accum_out=seg_t[:, c:c + 1]))
            dve.wait_ge(dve_step, n)
            n = mark(v.tensor_scalar(run_step[:, 1:5], seg_t[:, 0:4], -1.0, 2.0 * TPAD, ALU.mult, ALU.add))
            link(v.tensor_tensor_scan(tile0[:, 1:6], ones[:, 0:5], seg_t[:, :], 0.0, ALU.mult, ALU.add))
            n = mark(v.scalar_tensor_tensor(out=tile_p[:, 0:5], in0=tile0[:, 0:5], scalar=iota_p[:, 0:1],
                                            in1=run_step[:, :], op0=ALU.is_le, op1=ALU.mult, accum_out=run_base[:, :]))
            link(v.tensor_scalar(tile_p[:, 5:10], tile0[:, 0:5], iota_p[:, 0:1], None, ALU.is_le, ALU.add,
                                 accum_out=chunk_p[:, :]))
            for a in range(2):
                n = mark(v.tensor_scalar(run_idx[:, a:a + 1], run_base[:, :], iota_p[:, 0:1], float(a * TPAD),
                                         ALU.add, ALU.add))
            dve.wait_ge(dve_step, n)
            v.tensor_scalar(chunk_p[:, :], chunk_p[:, :], -1.0, float(P), ALU.add, ALU.mult).then_inc(tile_tables, 1)
            link(v.tensor_scalar(ct[:, :], iota_t[0:HEADS, :], tile0[0:HEADS, 1:2], None, ALU.is_ge))
            for c in range(2, CHUNKS):
                link(v.scalar_tensor_tensor(out=ct[:, :], in0=iota_t[0:HEADS, :], scalar=tile0[0:HEADS, c:c + 1],
                                            in1=ct[:, :], op0=ALU.is_ge, op1=ALU.add))
            v.tensor_copy(ct_i[:, :], ct[0:1, :]).then_inc(tile_tables, 1)

            dve.wait_ge(flag_ready, 1)
            unsorted = dve.value_load(flag_i[0:1, 0:1], min_val=0, max_val=EDGES)
            with dve.If(unsorted > 0):
                dve.wait_ge(rank_cols, 32)
                dve.wait_ge(rank_iota, 2)
                v.tensor_copy(rk_kcol, rk_col_i[:, 1, :]).then_inc(rank_iota, 1)
                dve.wait_ge(rank_iota, 3)
                v.scalar_tensor_tensor(out=rk_kcol, in0=rk_kcol, scalar=SORT_SHIFT, in1=rk_eno,
                                       op0=ALU.mult, op1=ALU.add).then_inc(rank_iota, 1)
                for b in range(RBLOCKS):
                    dve.wait_ge(rank_blk, 16 * (b + 1))
                    dve.wait_ge(rank_iota, 4 + 3 * b)
                    v.tensor_copy(rk_key, rk_int).then_inc(rank_iota, 1)
                    dve.wait_ge(rank_iota, 5 + 3 * b)
                    v.scalar_tensor_tensor(out=rk_key, in0=rk_key, scalar=SORT_SHIFT, in1=rk_iota,
                                           op0=ALU.mult, op1=ALU.add).then_inc(rank_iota, 1)
                    dve.wait_ge(rank_iota, 6 + 3 * b)
                    with dve.Fori(0, ETILES) as t:
                        v.tensor_scalar(rk_out, rk_key, rk_kcol[:, bass.ds(t, 1)], None, ALU.is_lt, ALU.add,
                                        accum_out=rk_cnt[:, bass.ds(t + b * ETILES, 1)]).then_inc(rank_tile, 1)
                        dve.wait_ge(rank_tile, t + (1 + b * ETILES))
                    v.tensor_scalar(rk_kcol, rk_kcol, float(-RB), None, ALU.add).then_inc(rank_iota, 1)
                    dve.wait_ge(rank_iota, 7 + 3 * b)
                    v.tensor_copy(scrap[0:1, 0:1], rk_kcol[0:1, 0:1]).then_inc(rank_used, 1)
                dve.wait_ge(rank_used, RBLOCKS)
                v.tensor_reduce(rk_pos, rk_cnt.rearrange("p (b t) -> p t b", b=RBLOCKS), AX_X, ALU.add
                                ).then_inc(rank_iota, 1)
                dve.wait_ge(rank_iota, 5 + 3 * RBLOCKS)
                v.tensor_copy(rk_pos_i[:, 0, :], rk_pos).then_inc(rank_iota, 1)
                v.tensor_scalar(rk_pos_i[:, 1, :], rk_pos, float(STAGE), None, ALU.add).then_inc(ranked, 1)
            link(v.memset(cont[:, 0:1], 0.0))

            def evacuate(l, k):
                (kind, c), b = ORDER[l][k], k % 2
                row, bias = stage_f[:, kind, :], (bias_s, bias_d)[kind]
                if k == 0:
                    dve.wait_ge(bias_in, 32 * (l + 1))
                    dve.wait_ge(attn_in, 16 * (l + 1))
                dve.wait_ge(proj_ready[b], CHUNKS * l + k // 2 + 1)
                if c > 0 or l > 0:
                    dve.wait_ge(*((table_stored, 16 * (CHUNKS * l + c)), (fd_ready, CHUNKS * l + c))[kind])
                v.tensor_tensor(row[:, 0:DIM].rearrange("p (a n) -> p a n", a=2),
                                ps[:, b * 1024:(b + 1) * 1024].rearrange("p (a n) -> p a n", a=2)[:, :, 0:HALF],
                                bias[:, :].rearrange("p (a n) -> p a n", a=2), ALU.add).then_inc(proj_free[b], 1)
                dve.wait_ge(proj_free[b], CHUNKS * l + k // 2 + 1)
                by_head = prod.rearrange("p (h d) -> p h d", h=HEADS)
                if kind == SRC:
                    link(v.tensor_tensor(prod, row[:, 0:DIM], attn[:, :], ALU.mult))
                    v.tensor_reduce(row[:, DIM:ROW], by_head, AX_X, ALU.add).then_inc(row_ready[0], 1)
                    return
                multiplied = mark(v.tensor_tensor(prod, row[:, 0:DIM], attn[:, :], ALU.mult))
                p0, p1, p2 = (fd3[:, c, a, :] for a in range(3))
                dve.wait_ge(fd_part, 2 * (CHUNKS * l + c) + 1)
                v.tensor_tensor(row[:, 0:DIM], row[:, 0:DIM], p0[:, 0:DIM], ALU.subtract).then_inc(row_ready[1], 1)
                dve.wait_ge(dve_step, multiplied)
                tail = slice(DIM, ROW)
                link(v.tensor_reduce(row[:, tail], by_head, AX_X, ALU.add))
                link(v.tensor_copy(p0[:, tail], row[:, tail]))
                link(v.tensor_tensor(row[:, tail], row[:, tail], p0[:, tail], ALU.subtract))
                link(v.tensor_copy(p1[:, tail], row[:, tail]))
                v.tensor_tensor(p2[:, tail], row[:, tail], p1[:, tail], ALU.subtract)
                dve.wait_ge(fd_part, 2 * (CHUNKS * l + c) + 2)
                v.tensor_tensor(p2[:, 0:DIM], row[:, 0:DIM], p1[:, 0:DIM], ALU.subtract).then_inc(fd_ready, 1)

            def tile_rows():
                dve.wait_ge(rows_in, 32)
                dve.wait_ge(tile_tables, 2)
                v.tensor_copy(rows_f[:, 0, :], rows_i[:, 0, :]).then_inc(rows_conv, 1)
                v.tensor_scalar(rows_f[:, 1, :], rows_i[:, 1, :], chunk_p[0:TPAD, 0:1], None, ALU.subtract
                                ).then_inc(rows_conv, 1)
                dve.wait_ge(rows_conv, 2)
                for a, e in ((0, 0), (1, P - 1)):
                    v.tensor_copy(end_cols[:, a, :], rows_f[:, 1, e:e + 1].to_broadcast([TPAD, HEADS])
                                  ).then_inc(rows_conv, 1)
                v.tensor_copy(rel_b[:, :], rows_f[:, 1, :]).then_inc(rows_conv, 1)

            def tile_columns():
                n = TPAD
                dve.wait_ge(rows_turned, 1)
                v.tensor_copy(src_i[:, :], ps[:, SRC_PS:SRC_PS + n]).then_inc(src_ready, 1)
                link(v.tensor_copy(dst_rel[:, :], ps[:, DST_PS:DST_PS + n]))
                link(v.tensor_copy(ends[:, :, :], ps[0:HEADS, ENDS_PS:ENDS_PS + 2 * n].rearrange("p (a t) -> p a t", a=2)))
                dve.wait_ge(dst_spread, 1)
                v.tensor_copy(dst_ht[:, 0:3, :], ps[:, SPREAD_PS[0]:SPREAD_PS[0] + HALF]
                              .rearrange("p (g e) -> p g e", g=3)).then_inc(spread_copied, 1)
                link(v.tensor_tensor(single[:, :], ends[:, 0, :], ends[:, 1, :], ALU.is_equal))
                link(v.tensor_tensor(cont[:, 1:n], ends[:, 0, 1:n], ends[:, 1, 0:n - 1], ALU.is_equal))
                link(v.tensor_tensor(tmp_row[:, 1:n], ct[:, 1:n], ct[:, 0:n - 1], ALU.is_equal))
                link(v.tensor_tensor(cont[:, 1:n], cont[:, 1:n], tmp_row[:, 1:n], ALU.mult))
                cp = chain_pen
                link(v.memset(cp[:, :, :], 0.0))
                link(v.tensor_tensor(cp[:, 0, 1:n], single[:, 0:n - 1], cont[:, 1:n], ALU.mult))
                link(v.tensor_copy(cp[:, 1, 1:n], cont[:, 1:n]))
                link(v.tensor_tensor(cp[:, 2, 0:n - 1], single[:, 1:n], cont[:, 1:n], ALU.mult))
                link(v.tensor_copy(cp[:, 3, 0:n - 1], cont[:, 1:n]))
                link(v.tensor_scalar(cp[:, :, :], cp[:, :, :], -NO, NO, ALU.mult, ALU.add))

            def scan_penalties():
                dve.wait_ge(dst_spread, 2)
                v.tensor_copy(dst_ht[:, 3:6, :], ps[:, SPREAD_PS[1]:SPREAD_PS[1] + HALF]
                              .rearrange("p (g e) -> p g e", g=3)).then_inc(spread_copied, 1)
                dve.wait_ge(spread_copied, 2)
                d = dst_ht
                ends_of = lambda e: d[:, :, e:e + 1].to_broadcast([P, GROUPS, P])
                v.memset(pen[:, 0, :, 0:1], 1.0)
                v.memset(pen[:, 1, :, P - 1:P], 1.0)
                v.tensor_tensor(pen[:, 0, :, 1:P], d[:, :, 1:P], d[:, :, 0:P - 1], ALU.not_equal)
                v.tensor_tensor(pen[:, 1, :, 0:P - 1], d[:, :, 1:P], d[:, :, 0:P - 1], ALU.not_equal)
                v.tensor_tensor(pen[:, 2, :, :], d[:, :, :], ends_of(0), ALU.not_equal)
                link(v.tensor_tensor(pen[:, 3, :, :], d[:, :, :], ends_of(P - 1), ALU.not_equal))
                flat = pen[:, :, :, :].rearrange("p a g e -> p (a g e)")
                link(v.tensor_scalar(flat, flat, NO, None, ALU.mult))

            def fd_onehots():
                dve.wait_ge(dstbc_in, 16)
                v.tensor_scalar(ohT[:, :, :].rearrange("p t e -> p (t e)"), dst_bc, iota_p[:, 0:1], None,
                                ALU.is_equal).then_inc(ohT_ready, 1)

            def edge_logits(l):
                def turn(i, first):
                    for u in range(UN):
                        b = u % FB
                        g = u % GB
                        t = i * UN + u
                        dve.wait_ge(f_ready[b], nth(i, u, FB, 1 + TILES // FB * l))
                        dve.wait_ge(gathered[g], landed(i, u, 2 * l))
                        mid = b * 1024 + 512
                        at = mid - SPLIT[l]
                        rest = ps[:, mid:at + DIM]
                        v.tensor_tensor(rest, rest, gat[:, g, SPLIT[l]:DIM], ALU.add).then_inc(sum_ready, 1)
                        v.tensor_tensor(lin[:, bass.ds(t, 1), :].rearrange("p a h -> p (a h)"),
                                        ps[:, at + DIM:at + ROW], gat[:, g, DIM:ROW], ALU.add
                                        ).then_inc(g_free[g], 1)
                        if l == 0 and not (first and u == 0):
                            sum_heads(t - 1, (u - 1) % UN, i if u else i - 1)
                        weigh(i, t, u, first and u < 2)

                def weigh(i, t, u, early):
                    b = u % FB
                    dve.wait_ge(sum_ready, t + (1 + TILES * l))
                    if l == 0 and not early:
                        dve.wait_ge(heads_act, t - 1)
                    acc = dict(accum_out=relu_sum[:, bass.ds(t, 1), 0:1].rearrange("p a o -> p (a o)")) if l else {}
                    at = b * 1024 + 512 - SPLIT[l]
                    v.scalar_tensor_tensor(out=prods[:, u % 2, :], in0=ps[:, at:at + DIM], scalar=0.0,
                                           in1=attn[:, :], op0=ALU.max, op1=ALU.mult, **acc).then_inc(f_free[b], 1)

                def sum_heads(t, u, i):
                    dve.wait_ge(f_free[u % FB], nth(i, u, FB, 2))
                    v.tensor_reduce(relu_sum[:, bass.ds(t, 1), 0:DH].rearrange("p a h -> p (a h)"),
                                    prods[:, u % 2, 0:DH * HD].rearrange("p (h d) -> p h d", h=DH), AX_X, ALU.add
                                    ).then_inc(heads_dve, 1)

                turn(0, True)
                with dve.Fori(1, TURNS) as i:
                    turn(i, False)
                logits_of_half(l, 0)
                if l == 0:
                    sum_heads(TILES - 1, UN - 1, TURNS - 1)

            def logits_of_half(l, a):
                at = slice(a * HG * GT, (a + 1) * HG * GT)
                tiles = (HG * GT, TILES)[a]
                if l == 0:
                    dve.wait_ge(heads_dve, tiles)
                    dve.wait_ge(heads_act, tiles)
                for g in range(GB):
                    dve.wait_ge(g_free[g], (2 * l * TILES + tiles) // GB + 1)
                if l == 0:
                    v.scalar_tensor_tensor(out=logits[:, at, :], in0=lin[:, at, :],
                                           scalar=SLOPE / (1.0 - SLOPE), in1=relu_sum[:, at, :],
                                           op0=ALU.mult, op1=ALU.add).then_inc(logits_ready, 1)
                else:
                    for b in range(FB):
                        dve.wait_ge(f_free[b], (TILES + tiles) // FB + 1)
                    link(v.tensor_reduce(scrap[:, at], lin[:, at, :], AX_X, ALU.add))
                    v.scalar_tensor_tensor(
                        out=logits[:, at, 0], in0=scrap[:, at], scalar=SLOPE / (1.0 - SLOPE),
                        in1=relu_sum[:, at, 0], op0=ALU.mult, op1=ALU.add).then_inc(logits_ready, 1)

            def softmax(l):
                flat = lambda t, a: t[:, a * HG:(a + 1) * HG, :].rearrange("p g e -> p (g e)")
                turned_logits = lambda a: ps[:, a * 512:a * 512 + HALF]

                def forwards(a):
                    dve.wait_ge(logits_turned, 2 * l + a + 1)
                    return mark(v.tensor_tensor_scan(flat(mx, a), flat(pen[:, 0, :, :], a), turned_logits(a),
                                                     NO, ALU.add, ALU.max))

                def backwards(a):
                    return mark(v.tensor_tensor_scan(flat(mx2, a)[:, ::-1], flat(pen[:, 1, :, :], a)[:, ::-1],
                                                     flat(mx, a)[:, ::-1], NO, ALU.add, ALU.max))

                n = forwards(0)
                logits_of_half(l, 1)
                dve.wait_ge(dve_step, n)
                backwards(0)
                dve.wait_ge(dve_step, forwards(1))
                dve.wait_ge(dve_step, backwards(1))
                own_tile = tile_of[:, :].rearrange("p (o t) -> p o t", o=1)
                for a, e in ((0, P - 1), (1, 0)):
                    v.tensor_tensor(by_tile[:, a * GROUPS:(a + 1) * GROUPS, :],
                                    mx2[:, :, e:e + 1].to_broadcast([P, GROUPS, GT]),
                                    own_tile.to_broadcast([P, GROUPS, GT]), ALU.mult).then_inc(ends_split, 1)
                dve.wait_ge(ends_turned, l + 1)
                n = TPAD
                reach = [ps[0:HEADS, CHAIN_PS + a * n:CHAIN_PS + (a + 1) * n] for a in range(2)]
                mark(v.tensor_tensor(brow[:, 0, 1:n], reach[0][:, 0:n - 1], chain_pen[:, 1, 1:n], ALU.add))
                link(v.tensor_tensor(brow[:, 1, 0:n - 1], reach[1][:, 1:n], chain_pen[:, 3, 0:n - 1], ALU.add))
                v.tensor_tensor_scan(srow[:, 0, :], chain_pen[:, 0, :], brow[:, 0, :], NO, ALU.add, ALU.max
                                     ).then_inc(chain_ready, 1)
                v.tensor_tensor_scan(srow[:, 1, ::-1], chain_pen[:, 2, ::-1], brow[:, 1, ::-1],
                                     NO, ALU.add, ALU.max).then_inc(chain_ready, 1)
                dve.wait_ge(chain_spread, l + 1)
                link(v.tensor_tensor(by_tile, ps[:, CARRY_PS:CARRY_PS + 2 * n].rearrange("p (g t) -> p g t", t=GT),
                                     own_tile.to_broadcast([P, 2 * GROUPS, GT]), ALU.mult))
                link(v.tensor_reduce(carry, by_tile, AX_X, ALU.add))
                for a in range(2):
                    for side, (i0, o) in enumerate(((mx2, mx), (mx, mx2))):
                        for g in range(a * HG, (a + 1) * HG):
                            k = side * GROUPS + g
                            n = mark(v.scalar_tensor_tensor(
                                out=o[:, g, :], in0=pen[:, 2 + side, g, :], scalar=carry[:, k:k + 1],
                                in1=i0[:, g, :], op0=ALU.add, op1=ALU.max))
                        dve.wait_ge(dve_step, n)
                    v.tensor_tensor(flat(mx, a), turned_logits(a), flat(mx2, a), ALU.subtract).then_inc(shifted, 1)

            def aggregation_inputs(l):
                def split_ex(a):
                    at = slice(a * HG * GT, (a + 1) * HG * GT)
                    dve.wait_ge(ex_ready, 2 * l + a + 1)
                    e = ex[:, at, :] if l == 0 else ex[:, at, 0:1].to_broadcast([P, HG * GT, HEADS])
                    p0, p1, p2 = (ex3[:, at, k, :] for k in range(3))
                    link(v.tensor_copy(p0, e))
                    link(v.tensor_tensor(ex_rest[:, at, :], e, p0, ALU.subtract))
                    link(v.tensor_copy(p1, ex_rest[:, at, :]))
                    v.tensor_tensor(p2, ex_rest[:, at, :], p1, ALU.subtract).then_inc(ex_split, 1)

                def turn(i):
                    for u in range(UN):
                        b, g = u % AB, u % GB
                        t = i * UN + u
                        dve.wait_ge(agg_free[b], nth(i, u, AB, 1 + TILES // AB * l))
                        v.tensor_scalar(onehot_b[:, b, :], iota_f[:, :], dst_rel[:, bass.ds(t, 1)], None, ALU.is_equal)
                        if l == 0:
                            v.tensor_scalar(onehot[:, b, :], iota_f[:, :], dst_rel[:, bass.ds(t, 1)], None,
                                            ALU.is_equal)
                            dve.wait_ge(gathered[g], landed(i, u, 1))
                            v.tensor_tensor(prods[:, b, :].rearrange("p (h d) -> p h d", h=HEADS),
                                            gat[:, g, 0:DIM].rearrange("p (h d) -> p h d", h=HEADS),
                                            ex[:, bass.ds(t, 1), :].rearrange("p a h -> p h a")
                                            .to_broadcast([P, HEADS, HD]), ALU.mult).then_inc(agg_in[b], 1)
                        else:
                            dve.wait_ge(gathered[g], landed(i, u, 3))
                            v.tensor_scalar(onehot[:, b, :], iota_f[:, :], dst_rel[:, bass.ds(t, 1)],
                                            ex[:, bass.ds(t, 1), 0:1].rearrange("p a o -> p (a o)"),
                                            ALU.is_equal, ALU.mult).then_inc(agg_in[b], 1)

                for a, turns in enumerate(HALVES):
                    split_ex(a)
                    with dve.Fori(*turns) as i:
                        turn(i)

            def moments(c):
                for a in range(2):
                    n = mark(v.bn_stats(bn6[:, c, a, :], v_sb[:, c, a * HALF:(a + 1) * HALF]))
                dve.wait_ge(dve_step, n)
                return mark(v.bn_aggr(mv[:, c, :], bn6[:, c, :, :].rearrange("p a s -> p (a s)")))

            def inverse_deviation(cols):
                y, y2, ve = rstd[:, cols], newton[:, cols], var_e[:, cols]
                link(v.tensor_scalar(ve, mv[:, cols, 1], EPS, None, ALU.add))
                link(v.tensor_scalar(y.bitcast(I32), ve.bitcast(I32), -0.5, RSQRT_BITS, ALU.mult, ALU.add))
                for _ in range(3):
                    link(v.tensor_tensor(y2, y, y, ALU.mult))
                    link(v.scalar_tensor_tensor(out=y2, in0=y2, scalar=-0.5, in1=ve, op0=ALU.mult, op1=ALU.mult))
                    link(v.scalar_tensor_tensor(out=y, in0=y2, scalar=1.5, in1=y, op0=ALU.add, op1=ALU.mult))

            def divide(c):
                v.tensor_tensor(v_sb[:, c, :].rearrange("p (h d) -> p h d", h=HEADS),
                                ps[:, c * DIM:(c + 1) * DIM].rearrange("p (h d) -> p h d", h=HEADS),
                                rden[:, c * HEADS:(c + 1) * HEADS].rearrange("p (h o) -> p h o", o=1)
                                .to_broadcast([P, HEADS, HD]), ALU.mult).then_inc(normed[c], 1)

            def elu(l, c):
                dve.wait_ge(v_exp, CHUNKS * l + c + 1)
                pm = posm[:, c % EB, :]
                if l == 0 and c == 0:
                    dve.wait_ge(relu_ready, 1)
                    link(v.tensor_tensor(pm, pm, x_sb[:, 0, :], ALU.add))
                elif l == 0:
                    dve.wait_ge(pos_ready, c)
                else:
                    dve.wait_ge(relu_ready, CHUNKS + c + 1)
                v.scalar_tensor_tensor(out=v_sb[:, c, :], in0=ev[:, c % EB, :], scalar=1.0,
                                       in1=posm[:, c % EB, :], op0=ALU.min, op1=ALU.add).then_inc(elu_used, 1)

            def scale(c):
                return mark(v.scalar_tensor_tensor(out=v_sb[:, c, :], in0=v_sb[:, c, :], scalar=mv[:, c, 0:1],
                                                   in1=ln_w[:, :], op0=ALU.subtract, op1=ALU.mult))

            def shift(l, c):
                return v.scalar_tensor_tensor(out=v_sb[:, c, :], in0=v_sb[:, c, :], scalar=rstd[:, c:c + 1],
                                              in1=ln_b[:, :] if l == 0 else x_sb[:, c, :],
                                              op0=ALU.mult, op1=ALU.add)

            def norm(c):
                dve.wait_ge(elu_used, c + 1)
                dve.wait_ge(dve_step, moments(c))
                scaled = scale(c)
                inverse_deviation(slice(c, c + 1))
                dve.wait_ge(dve_step, scaled)
                shift(0, c).then_inc(h_ready, 1)

            def denominators(l):
                dve.wait_ge(agg_done, l + 1)
                link(v.tensor_reduce(rden[:, :].rearrange("p (c h) -> p c h", c=CHUNKS),
                                     ps[:, DEN:DEN + CHUNKS * 3 * HEADS].rearrange("p (c a h) -> p c h a", c=CHUNKS, a=3),
                                     AX_X, ALU.add))
                link(v.tensor_scalar(rden[:, :], rden[:, :], TINY, None, ALU.max))
                link(v.reciprocal(rden[:, :], rden[:, :]))

            def last_nodes():
                for c in range(CHUNKS):
                    elu(1, c)
                    if c > 0:
                        dve.wait_ge(elu_used, CHUNKS + c)
                        moments(c - 1)
                dve.wait_ge(elu_used, 2 * CHUNKS)
                dve.wait_ge(dve_step, moments(CHUNKS - 1))
                dve.wait_ge(norm_in, 64)
                for c in range(CHUNKS):
                    scaled = scale(c)
                inverse_deviation(slice(0, CHUNKS))
                dve.wait_ge(dve_step, scaled)
                dve.wait_ge(xb_ready, CHUNKS)
                for c in range(CHUNKS):
                    done = mark(shift(1, c))
                    if c > 0:
                        dve.wait_ge(dve_step, before)
                        moments(c - 1)
                    before = done
                dve.wait_ge(dve_step, before)
                dve.wait_ge(dve_step, moments(CHUNKS - 1))
                inverse_deviation(slice(0, CHUNKS))
                v.scalar_tensor_tensor(out=shift_by[:, :], in0=mv[:, :, 0], scalar=-1.0, in1=rstd[:, :],
                                       op0=ALU.mult, op1=ALU.mult).then_inc(last_scale, 1)
                for c in range(CHUNKS):
                    if c not in ACT_LAST:
                        v.tensor_scalar(v_sb[:, c, :], v_sb[:, c, :], mv[:, c, 0:1], rstd[:, c:c + 1],
                                        ALU.subtract, ALU.mult).then_inc(out_ready[c], 1)

            link(v.tensor_copy(spread, ident[0:TPAD, 0:TPAD].rearrange("p (t o) -> p t o", o=1)
                               .to_broadcast([TPAD, TPAD, HEADS])))
            for k in range(2 * CHUNKS):
                evacuate(0, k)
                if k == 1:
                    tile_rows()
                if k == 2:
                    tile_columns()
                if k == 3:
                    scan_penalties()
                if k == 6:
                    fd_onehots()
            edge_logits(0)
            softmax(0)
            aggregation_inputs(0)
            denominators(0)
            dve.wait_ge(norm_in, 32)
            for c in (0, 1, 4):
                divide(c)
            elu(0, 0)
            norm(0)
            for c in (2, 3):
                divide(c)
            for c in range(1, 3):
                elu(0, c)
                norm(c)
            evacuate(1, 0)
            elu(0, 3)
            norm(3)
            evacuate(1, 1)
            evacuate(1, 2)
            elu(0, 4)
            norm(4)
            for k in range(3, 2 * CHUNKS):
                evacuate(1, k)
            edge_logits(1)
            softmax(1)
            aggregation_inputs(1)
            denominators(1)
            for c in range(CHUNKS):
                divide(c)
            last_nodes()

_INS = ['x', 'src', 'dst', 'L0_gnn_W1s', 'L0_gnn_b1s', 'L0_gnn_W1d', 'L0_gnn_b1d', 'L0_gnn_attn1',
        'L0_gnn_ln1_w', 'L0_gnn_ln1_b', 'L0_gnn_Wos', 'L0_gnn_bos', 'L0_gnn_Wod', 'L0_gnn_bod',
        'L0_gnn_attno', 'L0_gnn_lno_w', 'L0_gnn_lno_b']
_OUTS = [((NODES, DIM), 'float32')]


def kernel(**inputs):
    import numpy as _np
    import concourse.bacc as _bacc
    from concourse import mybir as _mybir
    from concourse.bass_utils import run_bass_kernel_spmd as _run

    nc = _bacc.Bacc("TRN2", target_bir_lowering=False, num_devices=1)
    arrays, args = {}, []
    for name in _INS:
        a = _np.ascontiguousarray(inputs[name])
        arrays[f"in_{name}_dram"] = a
        args.append(nc.dram_tensor(f"in_{name}_dram", a.shape, _mybir.dt.from_np(a.dtype), kind="ExternalInput").ap())
    for i, (shape, dtype) in enumerate(_OUTS):
        dt = _mybir.dt.from_np(_np.dtype(dtype))
        args.append(nc.dram_tensor(f"out_{i}_dram", shape, dt, kind="ExternalOutput").ap())
    gat_kernel(nc, *args)
    r = _run(nc, [arrays], core_ids=[0])
    got = tuple(r.results[0][f"out_{i}_dram"] for i in range(len(_OUTS)))
    return got[0]
```
